# Optimizing a Trainium2 kernel written in Bass

```python
import numpy as np
import jax
import jax.numpy as jnp

def _softmax(x, axis=-1):
    return jax.nn.softmax(x, axis=axis)

def _gelu(x):
    return jax.nn.gelu(x, approximate=True)

def _silu(x):
    return jax.nn.silu(x)

def _sigmoid(x):
    return jax.nn.sigmoid(x)

def _layernorm(x, axis=-1, eps=1e-05):
    m = jnp.mean(x, axis=axis, keepdims=True)
    v = jnp.var(x, axis=axis, keepdims=True)
    return (x - m) / jnp.sqrt(v + eps)

def _scatter_add(tgt, idx, src, axis=0):
    return tgt.at[idx].add(src)

def _segment_sum(src, seg, n):
    return jax.ops.segment_sum(src, seg, n)
kernel_name = 'mk_prb_d1_jaxref_r8_31189b'

def setup_inputs(seed: int=0):
    np.random.seed(seed)
    _w = jnp.asarray

    def _L0_attn_setup():
        import jax, jax.numpy as jnp
        import numpy as np
        import math
        D_MODEL = 128
        NUM_HEADS = 16
        HEAD_DIM = D_MODEL // NUM_HEADS
        ROPE_THETA = 10000.0

        def _rope_tables(seq_len, dim, theta=ROPE_THETA):
            inv = 1.0 / theta ** (jnp.arange(0, dim, 2, dtype=jnp.float32) / dim)
            t = jnp.arange(seq_len, dtype=jnp.float32)
            f = jnp.outer(t, inv)
            cos = jnp.repeat(jnp.cos(f), 2, axis=-1)
            sin = jnp.repeat(jnp.sin(f), 2, axis=-1)
            return (cos, sin)

        def _rotate_half(x):
            x1 = x[..., ::2]
            x2 = x[..., 1::2]
            return jnp.stack((-x2, x1), axis=-1).reshape(x.shape)
        key = jax.random.key(seed)
        ks = jax.random.split(key, 5)
        scale = 1.0 / math.sqrt(D_MODEL)
        return {'x': jax.random.normal(ks[0], (2, 256, D_MODEL), dtype=jnp.float32), 'W_Q': jax.random.normal(ks[1], (D_MODEL, D_MODEL), dtype=jnp.float32) * scale, 'W_K': jax.random.normal(ks[2], (D_MODEL, D_MODEL), dtype=jnp.float32) * scale, 'W_V': jax.random.normal(ks[3], (D_MODEL, D_MODEL), dtype=jnp.float32) * scale, 'W_O': jax.random.normal(ks[4], (D_MODEL, D_MODEL), dtype=jnp.float32) * scale}
    _L0_attn_in = _L0_attn_setup()

    def _L0_ffn_setup():
        import jax, jax.numpy as jnp
        import numpy as np
        B, S, H = (2, 256, 128)
        E_ROUTED = 8
        TOP_K = 2
        I = 256
        key = jax.random.key(seed)
        ks = jax.random.split(key, 9)
        s = 0.02
        return {'x': jax.random.normal(ks[0], (B, S, H), dtype=jnp.float32), 'shared_gate': jax.random.normal(ks[1], (I, H), dtype=jnp.float32) * s, 'shared_up': jax.random.normal(ks[2], (I, H), dtype=jnp.float32) * s, 'shared_down': jax.random.normal(ks[3], (H, I), dtype=jnp.float32) * s, 'gate_w': jax.random.normal(ks[4], (E_ROUTED, H, I), dtype=jnp.float32) * s, 'up_w': jax.random.normal(ks[5], (E_ROUTED, H, I), dtype=jnp.float32) * s, 'down_w': jax.random.normal(ks[6], (E_ROUTED, I, H), dtype=jnp.float32) * s, 'router_w': jax.random.normal(ks[7], (E_ROUTED, H), dtype=jnp.float32) * s, 'routing_bias': jnp.zeros((E_ROUTED,), dtype=jnp.float32)}
    _L0_ffn_in = _L0_ffn_setup()
    _d = {'L0_attn_x': _L0_attn_in['x'], 'L0_attn_W_Q': _L0_attn_in['W_Q'], 'L0_attn_W_K': _L0_attn_in['W_K'], 'L0_attn_W_V': _L0_attn_in['W_V'], 'L0_attn_W_O': _L0_attn_in['W_O'], 'L0_ffn_shared_gate': _L0_ffn_in['shared_gate'], 'L0_ffn_shared_up': _L0_ffn_in['shared_up'], 'L0_ffn_shared_down': _L0_ffn_in['shared_down'], 'L0_ffn_gate_w': _L0_ffn_in['gate_w'], 'L0_ffn_up_w': _L0_ffn_in['up_w'], 'L0_ffn_down_w': _L0_ffn_in['down_w'], 'L0_ffn_router_w': _L0_ffn_in['router_w'], 'L0_ffn_routing_bias': _L0_ffn_in['routing_bias']}
    _x0 = _d['L0_attn_x']
    _d['L0_attn_x'] = jax.random.normal(jax.random.fold_in(jax.random.key(seed), 1), (8, 256, 128), dtype=_x0.dtype)
    del _x0
    return _d

def reference(L0_attn_x, L0_attn_W_Q, L0_attn_W_K, L0_attn_W_V, L0_attn_W_O, L0_ffn_shared_gate, L0_ffn_shared_up, L0_ffn_shared_down, L0_ffn_gate_w, L0_ffn_up_w, L0_ffn_down_w, L0_ffn_router_w, L0_ffn_routing_bias):

    def _L0_attn_ref(x, W_Q, W_K, W_V, W_O):
        import jax, jax.numpy as jnp
        import numpy as np
        import math
        D_MODEL = 128
        NUM_HEADS = 16
        HEAD_DIM = D_MODEL // NUM_HEADS
        ROPE_THETA = 10000.0

        def _rope_tables(seq_len, dim, theta=ROPE_THETA):
            inv = 1.0 / theta ** (jnp.arange(0, dim, 2, dtype=jnp.float32) / dim)
            t = jnp.arange(seq_len, dtype=jnp.float32)
            f = jnp.outer(t, inv)
            cos = jnp.repeat(jnp.cos(f), 2, axis=-1)
            sin = jnp.repeat(jnp.sin(f), 2, axis=-1)
            return (cos, sin)

        def _rotate_half(x):
            x1 = x[..., ::2]
            x2 = x[..., 1::2]
            return jnp.stack((-x2, x1), axis=-1).reshape(x.shape)
        B, L, _ = x.shape

        def proj(W):
            return jnp.einsum('bld,ed->ble', x, W).reshape(B, L, NUM_HEADS, HEAD_DIM).transpose(0, 2, 1, 3)
        q, k, v = (proj(W_Q), proj(W_K), proj(W_V))
        cos, sin = _rope_tables(L, HEAD_DIM)
        cos = cos[None, None].astype(x.dtype)
        sin = sin[None, None].astype(x.dtype)
        q = q * cos + _rotate_half(q) * sin
        k = k * cos + _rotate_half(k) * sin
        scores = jnp.einsum('bhqd,bhkd->bhqk', q, k) / math.sqrt(HEAD_DIM)
        attn = jax.nn.softmax(scores, axis=-1)
        ctx = jnp.einsum('bhqk,bhkd->bhqd', attn, v)
        ctx = ctx.transpose(0, 2, 1, 3).reshape(B, L, D_MODEL)
        return jnp.einsum('bld,ed->ble', ctx, W_O)

    def _L0_ffn_ref(x, shared_gate, shared_up, shared_down, gate_w, up_w, down_w, router_w, routing_bias):
        import jax, jax.numpy as jnp
        import numpy as np
        B, S, H = (2, 256, 128)
        E_ROUTED = 8
        TOP_K = 2
        I = 256
        b, s, h = x.shape
        shared = jnp.einsum('bsi,hi->bsh', jax.nn.silu(jnp.einsum('bsh,ih->bsi', x, shared_gate)) * jnp.einsum('bsh,ih->bsi', x, shared_up), shared_down)
        logits = jnp.einsum('bsh,eh->bse', x, router_w) + routing_bias
        probs = jax.nn.sigmoid(logits)
        scores, indices = jax.lax.top_k(probs, TOP_K)
        scores = scores / jnp.sum(scores, axis=-1, keepdims=True)
        t = b * s
        xf = x.reshape(t, h)
        idx = indices.reshape(t, TOP_K)
        sc = scores.reshape(t, TOP_K)
        w = jnp.zeros((t, E_ROUTED), dtype=x.dtype)
        w = w.at[jnp.arange(t)[:, None], idx].add(sc)
        g = jax.nn.silu(jnp.einsum('th,ehi->tei', xf, gate_w))
        u = jnp.einsum('th,ehi->tei', xf, up_w)
        combined = jnp.einsum('tei,eih,te->th', g * u, down_w, w)
        return shared + combined.reshape(b, s, h)
    x = L0_attn_x
    xn = _layernorm(x, axis=-1)
    x = x + _L0_attn_ref(xn, L0_attn_W_Q, L0_attn_W_K, L0_attn_W_V, L0_attn_W_O) + _L0_ffn_ref(xn, L0_ffn_shared_gate, L0_ffn_shared_up, L0_ffn_shared_down, L0_ffn_gate_w, L0_ffn_up_w, L0_ffn_down_w, L0_ffn_router_w, L0_ffn_routing_bias)
    return x

_drawn_inputs = setup_inputs


def setup_inputs(seed=0):
    import zlib

    import numpy as np

    out = dict(_drawn_inputs(seed))
    spreads = {'L0_ffn_routing_bias': (0.0, 0.8)}
    factors = {'L0_ffn_shared_gate': 6.531,
     'L0_ffn_shared_up': 6.215,
     'L0_ffn_shared_down': 6.148,
     'L0_ffn_gate_w': 8.0,
     'L0_ffn_up_w': 8.0,
     'L0_ffn_down_w': 8.0,
     'L0_ffn_router_w': 8.0}
    for name, (base, spread) in spreads.items():
        noise = np.random.default_rng([zlib.crc32(name.encode()), seed]).standard_normal(out[name].shape)
        drawn = base * np.exp(spread * noise) if base else spread * noise
        out[name] = jnp.asarray(drawn.astype(out[name].dtype))
    for name, factor in factors.items():
        out[name] = (out[name] * factor).astype(out[name].dtype)
    return out
```

```python
import concourse.bass as bass
from concourse import mybir
from contextlib import ExitStack


def attention_moe_kernel(nc, x, w_proj, w_gu, w_dn, r_bias, rope, pick, k_one, eye, out, w_scratch):
    fp32 = mybir.dt.float32
    fr = mybir.dt.float32r
    ALU = mybir.AluOpType
    ACT = mybir.ActivationFunctionType
    AX = mybir.AxisListType

    TOK, D = x.shape
    NE = 8
    NX = NE + 1
    BLK = 512
    NB = TOK // BLK
    T = TOK // 128
    TB = BLK // 128
    SEQ = 256
    HEADS, HD = 16, 8
    SCALE = HD ** -0.5
    UNITS = 2 * NX
    AU = 14
    EPS = 1e-5
    PQ, PQS, PK, PKS, PV, PO, PR = [128 * n for n in range(7)]
    WP = w_proj.shape[1]
    TERMS = 3 * HD
    TERMS_MAX = TERMS + 2

    with ExitStack() as ctx:
        def sb(name, shape, dt=fp32):
            return ctx.enter_context(nc.sbuf_tensor(name, shape, dt))

        def sem(name):
            return ctx.enter_context(nc.semaphore(name))

        xh = sb("xh", [128, TOK], fr)
        xl = sb("xl", [128, TOK], fr)
        wp_h = sb("wp_h", [128, WP], fr)
        wp_l = sb("wp_l", [128, WP], fr)
        gu_h = sb("gu_h", [128, NX, 512], fr)
        gu_l = sb("gu_l", [128, NX, 512], fr)
        dn = sb("dn", [128, NX, 2, 128])
        sel = sb("sel", [128, 16, 128], fr)
        rope_t = sb("rope_t", [128, 2, BLK])
        ident = sb("ident", [128, 128])
        kone = sb("kone", [128, 1])
        v_all = sb("v_all", [128, T, 128])
        v_aug = sb("v_aug", [128, TB, HEADS, 32])
        qst = sb("qst", [128, 4, BLK], fr)
        kst = sb("kst", [128, 4, BLK], fr)
        mx = sb("mx", [128, 128])
        nmh = sb("nmh", [64, 128], fr)
        nml = sb("nml", [64, 128], fr)
        pt = sb("pt", [128, 2, 4, 2, 512])
        sg = sb("sg", [128, 2, 512])
        hb_ = sb("hidden", [128, 3, 512])
        wbc = sb("wbc", [128, NE, BLK])
        t1 = sb("t1", [128, BLK])
        t2 = sb("t2", [128, BLK])
        vh = sb("vh", [128, 2, BLK], fr)
        vl = sb("vl", [128, 2, BLK], fr)
        cx = sb("cx", [128, 4, BLK])
        cn = sb("cn", [128, TB, 128])
        ch = sb("ch", [128, BLK], fr)
        cl = sb("cl", [128, BLK], fr)
        rc = sb("rc", [128, TB, 16])
        xres = sb("xres", [128, TB, 128])
        st = sb("st", [128, T, 6])
        mv = sb("mv", [128, T, 2])
        sm = sb("sm", [128, 4, T])
        rbias = sb("rbias", [128, NE])
        rt = sb("rt", [128, 6, T * NE])
        rsum = sb("rsum", [128, 2, T])
        flat = pt.rearrange("p a b c d -> p (a b c d)")
        gu_raw = flat[:, 0:NX * 512].rearrange("p (e n) -> p e n", e=NX)
        sel_raw = flat[:, NX * 512:NX * 512 + 2048].rearrange("p (a n) -> p a n", a=16)
        wp_raw = flat[:, NX * 512 + 2048:NX * 512 + 2048 + WP]
        x_raw = cx.rearrange("p a n -> p (a n)").rearrange("p (t d) -> p t d", t=T)
        xn = v_aug.rearrange("p t h c -> p (t h c)").rearrange("p (t d) -> p t d", t=T)
        cmp_ = hb_.rearrange("p a n -> p (a n)")[:, 0:NE * T * NE].rearrange("p (f t e) -> p f t e", f=NE, t=T)
        fin = cn.rearrange("p t n -> p (t n)")

        sc = ctx.enter_context(nc.psum_tensor("sc", [128, 4, 512], fp32))
        gu_p = ctx.enter_context(nc.psum_tensor("gu_p", [128, 2, 512], fp32))
        acc = ctx.enter_context(nc.psum_tensor("acc", [128, 512], fp32))
        misc = ctx.enter_context(nc.psum_tensor("misc", [128, 512], fp32))

        ld_x = [sem(f"ld_x{j}") for j in range(4)]
        ld_wp, ld_id, ld_c, ld_sel, ld_dn, ld_rb = (sem(n) for n in ("ld_wp", "ld_id", "ld_c", "ld_sel", "ld_dn", "ld_rb"))
        ld_gu = [sem(f"ld_gu{j}") for j in range(3)]
        ld_res, ld_w = sem("ld_res"), [sem(f"ld_w{e}") for e in range(NE)]
        dve_chain, mx0_ok = sem("dve_chain"), sem("mx0_ok")
        var_ok, sd_ok, xn_ok, xt_ok, xh_ok, xl_ok = (sem(n) for n in ("var_ok", "sd_ok", "xn_ok", "xt_ok", "xh_ok", "xl_ok"))
        wph_ok, wpl_ok, guh_ok, gul_ok, sel_ok, ones_ok = (sem(n) for n in ("wph_ok", "wpl_ok", "guh_ok", "gul_ok", "sel_ok", "ones_ok"))
        rt_ok, lg_ok, en_ok, w_ok, wt_ok, wts_ok, wst = (sem(n) for n in ("rt_ok", "lg_ok", "en_ok", "w_ok", "wt_ok", "wts_ok", "wst"))
        v_ok, vall_ok = sem("v_ok"), sem("vall_ok")
        proj_ok, rope_ok, qk_ok, vh_ok, vl_ok = (sem(n) for n in ("proj_ok", "rope_ok", "qk_ok", "vh_ok", "vl_ok"))
        pick_ok, qst_ok, kst_ok, vaug_ok = (sem(n) for n in ("pick_ok", "qst_ok", "kst_ok", "vaug_ok"))
        a_ok, mx_ok, mt_ok, nmh_ok, nml_ok, mrow_ok = (sem(n) for n in ("a_ok", "mx_ok", "mt_ok", "nmh_ok", "nml_ok", "mrow_ok"))
        b_ok, ex_ok, pv_ok, cx_ok, ct_ok, rc_ok, cn_ok = (sem(n) for n in ("b_ok", "ex_ok", "pv_ok", "cx_ok", "ct_ok", "rc_ok", "cn_ok"))
        cnt_ok, ch_ok, cl_ok, f_ok, ft_ok, o_ok, st_out = (sem(n) for n in ("cnt_ok", "ch_ok", "cl_ok", "f_ok", "ft_ok", "o_ok", "st_out"))
        g_ok, u_ok, silu_ok, h_ok, hw_ok, down_ok = (sem(n) for n in ("g_ok", "u_ok", "silu_ok", "h_ok", "hw_ok", "down_ok"))

        x_v = x.rearrange("(t p) d -> p t d", p=128)
        out_v = out.rearrange("(t p) d -> p t d", p=128)

        def tok(n):
            return bass.ds(n * BLK, BLK)

        def after(eng, sem_, count):
            if not isinstance(count, int) or count > 0:
                eng.wait_ge(sem_, count)

        def bank_of(w, hb):
            return (4 * w + hb) % 4

        block = ctx.enter_context(nc.Block())

        @block.sync
        def _(sp):
            for j in range(4):
                sp.dma_start(x_raw[:, 4 * j:4 * j + 4, :], x_v[:, 4 * j:4 * j + 4, :]).then_inc(ld_x[j], 16)
            sp.dma_start(ident[:, :], eye).then_inc(ld_id, 16)
            sp.dma_start(rbias[:, :], r_bias.rearrange("(a e) -> a e", a=1).to_broadcast([128, NE])).then_inc(ld_rb, 16)
            sp.dma_start(rope_t[:, :, :], rope).then_inc(ld_c, 16)
            sp.dma_start(kone[:, :], k_one).then_inc(ld_c, 16)
            sp.dma_start(dn[:, :, :, :], w_dn).then_inc(ld_dn, 16)
            sp.dma_start(xres[:, :, :], x_v[:, 0:TB, :]).then_inc(ld_res, 16)
            sp.wait_ge(wts_ok, 1)
            sp.dma_start(w_scratch.rearrange("e (t p) -> (e t) p", p=128), rt[:, 5, :]).then_inc(wst, 16)
            sp.wait_ge(wst, 16)

            def weights(e, n):
                sp.dma_start(wbc[:, e, :], w_scratch[e:e + 1, tok(n)].to_broadcast([128, BLK])).then_inc(ld_w[e], 16)

            for e in range(NE):
                weights(e, 0)

            def body(it, last):
                if not last:
                    for e in range(3):
                        sp.wait_ge(hw_ok, it * 16 + 2 * (e + 1))
                        weights(e, it + 1)
                sp.wait_ge(nml_ok, it + 1)
                sp.wait_ge(nmh_ok, it + 1)
                sp.dma_start(qst.bitcast(fp32)[TERMS:TERMS + 97:32, :, :], nmh.bitcast(fp32)[:, :]).then_inc(mrow_ok, 16)
                sp.dma_start(qst.bitcast(fp32)[TERMS + 1:TERMS + 98:32, :, :], nml.bitcast(fp32)[:, :]).then_inc(mrow_ok, 16)
                if not last:
                    for e in range(3, NE):
                        sp.wait_ge(hw_ok, it * 16 + 2 * (e + 1))
                        weights(e, it + 1)
                sp.wait_ge(o_ok, it + 1)
                sp.dma_start(out_v[:, bass.ds(it * TB, TB), :], xres[:, :, :]).then_inc(st_out, 16)
                sp.wait_ge(st_out, it * 16 + 16)
                if not last:
                    sp.dma_start(xres[:, :, :], x_v[:, bass.ds((it + 1) * TB, TB), :]).then_inc(ld_res, 16)

            body(0, False)
            with sp.Fori(1, NB - 1) as it:
                body(it, False)
            body(NB - 1, True)

        @block.gpsimd
        def _(pool):
            def rope_sum(n, w):
                pool.wait_ge(rope_ok, n * 2 + w + 1)
                pool.tensor_tensor(t1[:, :], t1[:, :], t2[:, :], ALU.add).then_inc(qk_ok, 1)

            def low_part(n, w):
                pool.wait_ge(vh_ok, n * 2 + w + 1)
                pool.tensor_tensor(vl[:, w, :], t1[:, :], vh.bitcast(fp32)[:, w, :], ALU.subtract).then_inc(vl_ok, 1)

            def values(n):
                after(pool, pv_ok, n * 4)
                pool.tensor_copy(v_aug[:, :, :, 0:HD], v_all[:, bass.ds(n * TB, TB), :].rearrange("p t (h d) -> p t h d", d=HD)).then_inc(vaug_ok, 1)

            pool.wait_ge(wph_ok, 1)
            pool.tensor_tensor(wp_l[:, :], wp_raw, wp_h.bitcast(fp32)[:, :], ALU.subtract).then_inc(wpl_ok, 1)
            rope_sum(0, 0)
            low_part(0, 0)
            rope_sum(0, 1)
            low_part(0, 1)
            for e in range(NX):
                pool.wait_ge(guh_ok, e + 1)
                pool.tensor_tensor(gu_l[:, e, :], gu_raw[:, e, :], gu_h.bitcast(fp32)[:, e, :], ALU.subtract).then_inc(gul_ok, 1)
                if e == 1:
                    pool.wait_ge(xt_ok, 4)
                    pool.memset(v_aug[:, :, :, :], 1.0).then_inc(ones_ok, 1)
                    pool.wait_ge(ones_ok, 1)
                    pool.wait_ge(vall_ok, 4)
                    values(0)

            def weigh(it, u):
                e = u // 2 - 1
                pool.wait_ge(h_ok, it * UNITS + u + 1)
                pool.wait_ge(ld_w[e], it * 16 + 16)
                pool.tensor_tensor(hb_[:, u % 3, :], hb_[:, u % 3, :], wbc[:, e, :], ALU.mult).then_inc(hw_ok, 1)

            def body(it, last):
                for u in range(2, UNITS):
                    weigh(it, u)
                    if not last and u == 10:
                        rope_sum(it + 1, 0)
                    if not last and u == 11:
                        low_part(it + 1, 0)
                    if not last and u == 12:
                        rope_sum(it + 1, 1)
                    if not last and u == 13:
                        low_part(it + 1, 1)
                    if not last and u == 15:
                        values(it + 1)

            body(0, False)
            with pool.Fori(1, NB - 1) as it:
                body(it, False)
            body(NB - 1, True)

        @block.scalar
        def _(act):
            act.dma_start(wp_raw, w_proj).then_inc(ld_wp, 16)
            act.dma_start(sel_raw, pick).then_inc(ld_sel, 16)
            for j in range(3):
                act.dma_start(gu_raw[:, 3 * j:3 * j + 3, :], w_gu[:, 3 * j:3 * j + 3, :]).then_inc(ld_gu[j], 16)
            act.wait_ge(ld_wp, 16)
            act.activation(wp_h[:, :], wp_raw, ACT.Copy).then_inc(wph_ok, 1)
            act.wait_ge(var_ok, 1)
            act.activation(sm[:, 1, :], sm[:, 0, :], ACT.Sqrt).then_inc(sd_ok, 1)
            act.wait_ge(ld_sel, 16)
            act.activation(sel[:, :, :], sel_raw, ACT.Copy).then_inc(sel_ok, 1)
            for j in range(4):
                act.wait_ge(xt_ok, j + 1)
                act.activation(xh[:, tok(j)], sc[:, j, :], ACT.Copy).then_inc(xh_ok, 1)
            for e in range(2):
                act.wait_ge(ld_gu[0], 16)
                act.activation(gu_h[:, e, :], gu_raw[:, e, :], ACT.Copy).then_inc(guh_ok, 1)
            for j in range(4):
                act.wait_ge(v_ok, j + 1)
                act.activation(v_all[:, 4 * j:4 * j + 4, :], sc[:, j, :], ACT.Copy).then_inc(vall_ok, 1)

            def high_part(n, w):
                act.wait_ge(qk_ok, n * 2 + w + 1)
                after(act, pick_ok, n * 8)
                act.activation(vh[:, w, :], t1[:, :], ACT.Copy).then_inc(vh_ok, 1)

            def k_rows(n, hb):
                act.wait_ge(pick_ok, n * 8 + 4 + hb + 1)
                act.activation(kst[:, hb, :], sc[:, bank_of(1, hb), :], ACT.Identity, bias=kone[:, 0:1]).then_inc(kst_ok, 1)

            high_part(0, 0)
            high_part(0, 1)
            act.wait_ge(lg_ok, 1)
            act.activation(rt[:, 1, :], rt[:, 0, :], ACT.Exp, scale=-1.0).then_inc(en_ok, 1)
            act.wait_ge(ld_c, 32)
            for hb in range(4):
                k_rows(0, hb)
            for e in range(2, NX):
                act.wait_ge(ld_gu[e // 3], 16)
                act.activation(gu_h[:, e, :], gu_raw[:, e, :], ACT.Copy).then_inc(guh_ok, 1)
            act.wait_ge(wt_ok, 1)
            act.activation(rt[:, 5, :], misc[:, 0:128], ACT.Copy).then_inc(wts_ok, 1)
            act.wait_ge(gul_ok, NX)

            def silu(it, u):
                act.wait_ge(g_ok, it * UNITS + u + 1)
                after(act, h_ok, it * UNITS + max(u - 1, 0))
                act.activation(sg[:, u % 2, :], gu_p[:, 0, :], ACT.Silu).then_inc(silu_ok, 1)

            def body(it, last):
                for u in range(AU):
                    silu(it, u)
                    if u == 9:
                        act.wait_ge(mt_ok, it + 1)
                        after(act, mrow_ok, it * 32)
                        act.activation(nmh[:, :], misc[0:64, 0:128], ACT.Copy, scale=-1.0).then_inc(nmh_ok, 1)
                    if not last and u == 11:
                        high_part(it + 1, 0)
                    if not last and u == 13:
                        high_part(it + 1, 1)
                for p in range(16):
                    hb, g = p // 4, p % 4
                    act.wait_ge(b_ok, it * 16 + p + 1)
                    after(act, pv_ok, it * 4 + max(hb - 1, 0))
                    act.activation(pt[:, hb % 2, g, :, :], sc[:, 2 * (p % 2):2 * (p % 2) + 2, :], ACT.Exp, scale=SCALE).then_inc(ex_ok, 1)
                silu(it, 14)
                silu(it, 15)
                act.wait_ge(cnt_ok, it + 1)
                act.activation(ch[:, :], misc[:, :], ACT.Copy).then_inc(ch_ok, 1)
                silu(it, 16)
                silu(it, 17)
                if not last:
                    for hb in range(4):
                        k_rows(it + 1, hb)
                act.wait_ge(down_ok, it * UNITS + UNITS)
                act.activation(fin, acc[:, :], ACT.Copy).then_inc(f_ok, 1)

            body(0, False)
            with act.Fori(1, NB - 1) as it:
                body(it, False)
            body(NB - 1, True)

        @block.vector
        def _(dve):
            chain = [0]

            def link(ins):
                chain[0] += 1
                ins.then_inc(dve_chain, 1)
                dve.wait_ge(dve_chain, chain[0])

            dve.memset(mx[:, :], 0.0).then_inc(mx0_ok, 1)
            for t in range(T):
                dve.wait_ge(ld_x[t // 4], 16)
                last_st = dve.bn_stats(st[:, t, :], x_raw[:, t, :])
            link(last_st)
            for t in range(T):
                last_mv = dve.bn_aggr(mv[:, t, :], st[:, t, :])
            link(last_mv)
            dve.tensor_scalar(sm[:, 0, :], mv[:, :, 1], EPS, None, ALU.add).then_inc(var_ok, 1)
            dve.wait_ge(sd_ok, 1)
            link(dve.reciprocal(sm[:, 2, :], sm[:, 1, :]))
            link(dve.tensor_tensor(sm[:, 1, :], sm[:, 2, :], sm[:, 2, :], ALU.mult))
            link(dve.tensor_tensor(sm[:, 3, :], sm[:, 1, :], sm[:, 0, :], ALU.mult))
            link(dve.tensor_scalar(sm[:, 1, :], sm[:, 3, :], -0.5, 1.5, ALU.mult, ALU.add))
            link(dve.tensor_tensor(sm[:, 3, :], sm[:, 1, :], sm[:, 2, :], ALU.mult))
            for t in range(T):
                dve.tensor_scalar(xn[:, t, :], x_raw[:, t, :], mv[:, t, 0:1], sm[:, 3, t:t + 1], ALU.subtract, ALU.mult).then_inc(xn_ok, 1)
            for j in range(4):
                dve.wait_ge(xh_ok, j + 1)
                dve.tensor_tensor(xl[:, tok(j)], sc[:, j, :], xh.bitcast(fp32)[:, tok(j)], ALU.subtract).then_inc(xl_ok, 1)

            def rotate(n, w):
                dve.wait_ge(proj_ok, n * 2 + w + 1)
                after(dve, vl_ok, n * 2 + w)
                dve.tensor_tensor(t1[:, :], gu_p[:, 0, :], rope_t[:, 0, :], ALU.mult)
                dve.tensor_tensor(t2[:, :], gu_p[:, 1, :], rope_t[:, 1, :], ALU.mult).then_inc(rope_ok, 1)

            def q_rows(n, hb):
                dve.wait_ge(pick_ok, n * 8 + hb + 1)
                dve.tensor_copy(qst[:, hb, :], sc[:, bank_of(0, hb), :]).then_inc(qst_ok, 1)

            dve.wait_ge(ld_c, 32)
            rotate(0, 0)
            rotate(0, 1)
            dve.wait_ge(rt_ok, 1)
            dve.wait_ge(ld_rb, 16)
            bias_b = rbias[:, :].rearrange("p (a e) -> p a e", a=1).to_broadcast([128, T, NE])
            te = lambda a: a.rearrange("p (t e) -> p t e", t=T)
            dve.tensor_tensor(te(rt[:, 0, :]), te(misc[:, 0:128]), bias_b, ALU.add).then_inc(lg_ok, 1)
            for hb in range(4):
                q_rows(0, hb)
            dve.wait_ge(en_ok, 1)
            link(dve.tensor_scalar(rt[:, 2, :], rt[:, 1, :], 1.0, None, ALU.add))
            link(dve.reciprocal(rt[:, 3, :], rt[:, 2, :]))
            prob = te(rt[:, 3, :])
            for f in range(NE):
                own = prob[:, :, f:f + 1]
                if f > 0:
                    last_c = dve.tensor_tensor(cmp_[:, f, :, 0:f], own.to_broadcast([128, T, f]), prob[:, :, 0:f], ALU.is_gt)
                last_c = dve.tensor_tensor(cmp_[:, f, :, f:NE], own.to_broadcast([128, T, NE - f]), prob[:, :, f:NE], ALU.is_ge)
            link(last_c)
            link(dve.tensor_reduce(te(rt[:, 0, :]), cmp_.rearrange("p f t e -> p t e f"), AX.X, ALU.add))
            link(dve.tensor_scalar(rt[:, 1, :], rt[:, 0, :], 2.5, None, ALU.is_lt))
            link(dve.tensor_tensor(rt[:, 2, :], rt[:, 1, :], rt[:, 3, :], ALU.mult))
            link(dve.tensor_reduce(rsum[:, 0, :], te(rt[:, 2, :]), AX.X, ALU.add))
            link(dve.reciprocal(rsum[:, 1, :], rsum[:, 0, :]))
            share = rsum[:, 1, :].rearrange("p (t a) -> p t a", a=1).to_broadcast([128, T, NE])
            dve.tensor_tensor(rt[:, 4, :].rearrange("p (e t) -> p t e", e=NE), te(rt[:, 2, :]), share, ALU.mult).then_inc(w_ok, 1)

            def hidden(it, u):
                dve.wait_ge(silu_ok, it * UNITS + u + 1)
                dve.wait_ge(u_ok, it * UNITS + u + 1)
                after(dve, down_ok, it * UNITS + max(u - 2, 0))
                dve.tensor_tensor(hb_[:, u % 3, :], gu_p[:, 1, :], sg[:, u % 2, :], ALU.mult).then_inc(h_ok, 1)

            def maxima(it, a):
                dve.wait_ge(a_ok, it * 16 + a + 1)
                dve.tensor_reduce(mx[:, 4 * a:4 * a + 4], sc[:, 2 * (a % 2):2 * (a % 2) + 2, :].rearrange("p b (q k) -> p (b q) k", q=2),
                                  AX.X, ALU.max).then_inc(mx_ok, 1)

            def body(it, last):
                for u in range(AU):
                    hidden(it, u)
                    if u == 0:
                        after(dve, mt_ok, it)
                    if u < 8:
                        maxima(it, 2 * u)
                        maxima(it, 2 * u + 1)
                    if u == 9:
                        dve.wait_ge(nmh_ok, it + 1)
                        dve.scalar_tensor_tensor(out=nml[:, :], in0=misc[0:64, 0:128], scalar=-1.0, in1=nmh.bitcast(fp32)[:, :],
                                                 op0=ALU.mult, op1=ALU.subtract).then_inc(nml_ok, 1)
                    if not last and u == 10:
                        rotate(it + 1, 0)
                    if not last and u == 12:
                        rotate(it + 1, 1)
                for hb in range(4):
                    dve.wait_ge(pv_ok, it * 4 + hb + 1)
                    after(dve, ct_ok, it * 4)
                    dve.tensor_copy(cx[:, hb, :], misc[:, :]).then_inc(cx_ok, 1)
                    if hb == 2:
                        hidden(it, 14)
                after(dve, ft_ok, it)
                for t in range(TB):
                    if t == 2:
                        hidden(it, 15)
                    dve.wait_ge(ct_ok, it * 4 + t + 1)
                    by_head = sc[:, t, :].rearrange("p (b g c) -> p b g c", g=4, c=32)
                    dve.reciprocal(rc[:, t, :].rearrange("p (b g) -> p b g", g=4), by_head[:, :, :, HD]).then_inc(rc_ok, 1)
                    dve.wait_ge(rc_ok, it * 4 + t + 1)
                    dve.tensor_tensor(cn[:, t, :].rearrange("p (g b d) -> p b g d", g=4, b=4), by_head[:, :, :, 0:HD],
                                      rc[:, t, :].rearrange("p (b g a) -> p b g a", g=4, a=1).to_broadcast([128, 4, 4, HD]),
                                      ALU.mult).then_inc(cn_ok, 1)
                dve.wait_ge(ch_ok, it + 1)
                dve.tensor_tensor(cl[:, :], misc[:, :], ch.bitcast(fp32)[:, :], ALU.subtract).then_inc(cl_ok, 1)
                hidden(it, 16)
                hidden(it, 17)
                if not last:
                    for hb in range(4):
                        q_rows(it + 1, hb)
                dve.wait_ge(ft_ok, it + 1)
                dve.wait_ge(ld_res, it * 16 + 16)
                dve.tensor_tensor(xres[:, :, :], misc[:, :].rearrange("p (t d) -> p t d", t=TB), xres[:, :, :], ALU.add).then_inc(o_ok, 1)

            body(0, False)
            with dve.Fori(1, NB - 1) as it:
                body(it, False)
            body(NB - 1, True)

        @block.tensor
        def _(pe):
            def three(dst, lhs_h, lhs_l, rhs_h, rhs_l, start=True, stop=True):
                pe.matmul(dst, lhs_h, rhs_h, start=start, stop=False)
                pe.matmul(dst, lhs_h, rhs_l, start=False, stop=False)
                return pe.matmul(dst, lhs_l, rhs_h, start=False, stop=stop)

            def wp(c, n=128):
                return wp_h[:, c:c + n], wp_l[:, c:c + n]

            def project(n, w):
                for s in range(2):
                    last = three(gu_p[:, s, :], *wp((2 * w + s) * 128), xh[:, tok(n)], xl[:, tok(n)])
                last.then_inc(proj_ok, 1)

            def pick_rows(n):
                for w in range(2):
                    pe.wait_ge(vl_ok, n * 2 + w + 1)
                    for hb in range(4):
                        if w == 1:
                            pe.wait_ge(qst_ok, n * 4 + hb + 1)
                        dst = sc[:, bank_of(w, hb), :]
                        pe.matmul(dst, sel[:, 8 * w + hb, :], vh[:, w, :], start=True, stop=False)
                        pe.matmul(dst, sel[:, 8 * w + 4 + hb, :], vl[:, w, :], start=False, stop=True).then_inc(pick_ok, 1)

            pe.wait_ge(ld_id, 16)
            pe.wait_ge(mx0_ok, 1)
            for j in range(4):
                for t in range(4 * j, 4 * j + 4):
                    pe.wait_ge(xn_ok, t + 1)
                    last = pe.transpose(sc[:, j, (t % 4) * 128:(t % 4) * 128 + 128], xn[:, t, :], ident[:, :])
                last.then_inc(xt_ok, 1)
            pe.wait_ge(wpl_ok, 1)
            pe.wait_ge(xl_ok, 1)
            project(0, 0)
            for t in range(T):
                pe.wait_ge(xl_ok, t // 4 + 1)
                cols = slice(128 * t, 128 * t + 128)
                last = three(misc[:, NE * t:NE * t + NE], xh[:, cols], xl[:, cols], *wp(PR, NE))
            last.then_inc(rt_ok, 1)
            pe.wait_ge(rope_ok, 1)
            project(0, 1)
            for j in range(4):
                for t in range(4 * j, 4 * j + 4):
                    cols = slice(128 * t, 128 * t + 128)
                    last = three(sc[:, j, (t % 4) * 128:(t % 4) * 128 + 128], xh[:, cols], xl[:, cols], *wp(PV))
                last.then_inc(v_ok, 1)
            pe.wait_ge(vall_ok, 4)
            pe.wait_ge(sel_ok, 1)
            pick_rows(0)
            pe.wait_ge(w_ok, 1)
            pe.transpose(misc[:, 0:128], rt[:, 4, :], ident[:, :]).then_inc(wt_ok, 1)
            pe.wait_ge(ld_dn, 16)
            pe.wait_ge(wts_ok, 1)
            pe.wait_ge(rope_ok, 2)

            def gate_up(it, u):
                e, c = u // 2, u % 2
                pe.wait_ge(gul_ok, e + 1)
                after(pe, silu_ok, it * UNITS + u)
                three(gu_p[:, 0, :], gu_h[:, e, c * 128:c * 128 + 128], gu_l[:, e, c * 128:c * 128 + 128],
                      xh[:, tok(it)], xl[:, tok(it)]).then_inc(g_ok, 1)
                after(pe, h_ok, it * UNITS + u)
                o = 256 + c * 128
                three(gu_p[:, 1, :], gu_h[:, e, o:o + 128], gu_l[:, e, o:o + 128],
                      xh[:, tok(it)], xl[:, tok(it)]).then_inc(u_ok, 1)

            def down(it, u):
                if u < 2:
                    pe.wait_ge(h_ok, it * UNITS + u + 1)
                else:
                    pe.wait_ge(hw_ok, it * 16 + u - 1)
                if u == 0:
                    after(pe, f_ok, it)
                last = pe.matmul(acc[:, :], dn[:, u // 2, u % 2, :], hb_[:, u % 3, :], start=(u == 0), stop=(u == UNITS - 1))
                last.then_inc(down_ok, 1)
                return last

            def scores(it, a):
                g, hb = a // 4, a % 4
                if a >= 2:
                    pe.wait_ge(mx_ok, it * 16 + a - 1)
                rows = slice(32 * g, 32 * g + TERMS)
                for b in range(2):
                    for qt in range(2):
                        q0 = b * SEQ + qt * 128
                        last = pe.matmul(sc[:, 2 * (a % 2) + b, qt * SEQ:qt * SEQ + SEQ], qst[rows, hb, q0:q0 + 128],
                                         kst[rows, hb, b * SEQ:b * SEQ + SEQ], start=True, stop=True)
                last.then_inc(a_ok, 1)

            def scores_t(it, p):
                hb, g = p // 4, p % 4
                if p >= 2:
                    pe.wait_ge(ex_ok, it * 16 + p - 1)
                rows = slice(32 * g, 32 * g + TERMS_MAX)
                for b in range(2):
                    for kt in range(2):
                        k0 = b * SEQ + kt * 128
                        last = pe.matmul(sc[:, 2 * (p % 2) + b, kt * SEQ:kt * SEQ + SEQ], kst[rows, hb, k0:k0 + 128],
                                         qst[rows, hb, b * SEQ:b * SEQ + SEQ], start=True, stop=True)
                last.then_inc(b_ok, 1)

            def context(it, hb):
                pe.wait_ge(ex_ok, it * 16 + 4 * hb + 4)
                if hb == 0:
                    pe.wait_ge(vaug_ok, it + 1)
                else:
                    pe.wait_ge(cx_ok, it * 4 + hb)
                for b in range(2):
                    for kt in range(2):
                        for g in range(4):
                            last = pe.matmul(misc[32 * g:32 * g + 32, b * SEQ:b * SEQ + SEQ], v_aug[:, 2 * b + kt, 4 * g + hb, :],
                                             pt[:, hb % 2, g, b, kt * SEQ:kt * SEQ + SEQ], start=(kt == 0), stop=(kt == 1))
                last.then_inc(pv_ok, 1)

            def body(it, last_block):
                for u in range(AU):
                    gate_up(it, u)
                    if u == 0:
                        pe.wait_ge(qst_ok, it * 4 + 4)
                        pe.wait_ge(kst_ok, it * 4 + 4)
                    if u < 8:
                        scores(it, 2 * u)
                        scores(it, 2 * u + 1)
                    if u >= 2:
                        down(it, u - 2)
                    if u == 9:
                        pe.wait_ge(mx_ok, it * 16 + 16)
                        after(pe, o_ok, it)
                        pe.transpose(misc[:, 0:128], mx[:, :], ident[:, :]).then_inc(mt_ok, 1)
                    if not last_block and u in (10, 12):
                        w = (u - 10) // 2
                        pe.wait_ge(silu_ok, it * UNITS + u + 1)
                        pe.wait_ge(h_ok, it * UNITS + u + 1)
                        project(it + 1, w)
                        pe.wait_ge(rope_ok, (it + 1) * 2 + w + 1)
                pe.wait_ge(mrow_ok, it * 32 + 32)
                pe.wait_ge(nml_ok, it + 1)
                for p in range(16):
                    scores_t(it, p)
                    if p == 1:
                        down(it, 12)
                    if p == 3:
                        down(it, 13)
                    if p >= 5 and p % 4 == 1:
                        context(it, p // 4 - 1)
                gate_up(it, 14)
                context(it, 3)
                gate_up(it, 15)
                pe.wait_ge(cx_ok, it * 4 + 4)
                for t in range(TB):
                    for hb in range(4):
                        last = pe.transpose(sc[:, t, hb * 128:hb * 128 + 128], cx[:, hb, t * 128:t * 128 + 128], ident[:, :])
                    last.then_inc(ct_ok, 1)
                down(it, 14)
                for t in range(TB):
                    pe.wait_ge(cn_ok, it * 4 + t + 1)
                    last = pe.transpose(misc[:, t * 128:t * 128 + 128], cn[:, t, :], ident[:, :])
                last.then_inc(cnt_ok, 1)
                down(it, 15)
                gate_up(it, 16)
                pe.wait_ge(cl_ok, it + 1)
                three(acc[:, :], *wp(PO), ch[:, :], cl[:, :], start=False, stop=False)
                gate_up(it, 17)
                down(it, 16)
                if not last_block:
                    pick_rows(it + 1)
                down(it, 17)

            def finish(it):
                pe.wait_ge(f_ok, it + 1)
                for t in range(TB):
                    last = pe.transpose(misc[:, t * 128:t * 128 + 128], fin[:, t * 128:t * 128 + 128], ident[:, :])
                last.then_inc(ft_ok, 1)

            body(0, False)
            finish(0)
            with pe.Fori(1, NB - 1) as it:
                body(it, False)
                finish(it)
            body(NB - 1, True)
            finish(NB - 1)


def _rope_tables():
    import numpy as np
    hd, seq = 8, 256
    inv = (1.0 / np.float32(10000.0) ** (np.arange(0, hd, 2, dtype=np.float32) / np.float32(hd))).astype(np.float32)
    ang = np.outer(np.arange(seq, dtype=np.float32), inv).astype(np.float32)
    cos, sin = np.cos(ang), np.sin(ang)
    table = np.zeros((128, 2, 512), np.float32)
    for e in range(128):
        i = (e % hd) // 2
        table[e, 0] = np.tile(cos[:, i], 2)
        table[e, 1] = np.tile(sin[:, i], 2) * (1.0 if e % 2 else -1.0)
    return table


def _row_picks():
    import numpy as np
    pick = np.zeros((128, 4, 4, 128), np.float32)
    parts = [(0, 1), (2,), (0, 2), (1,)]
    for kind, terms in enumerate(parts):
        for hb in range(4):
            for g in range(4):
                for d in range(8):
                    for j in terms:
                        pick[8 * (4 * g + hb) + d, kind, hb, 32 * g + 8 * j + d] = 1.0
    ones = np.zeros((128, 1), np.float32)
    for g in range(4):
        ones[32 * g + 24:32 * g + 26] = 1.0
    return pick.reshape(128, 16, 128), ones


def kernel(**inputs):
    import numpy as np
    import concourse.bacc as _bacc
    from concourse import mybir as _mybir
    from concourse.bass_utils import run_bass_kernel_spmd as _run

    g = {k.replace("L0_attn_", "").replace("L0_ffn_", ""): np.asarray(v) for k, v in inputs.items()}
    swap = np.arange(128).reshape(64, 2)[:, ::-1].reshape(-1)
    w_proj = np.concatenate([g["W_Q"].T, g["W_Q"][swap].T, g["W_K"].T, g["W_K"][swap].T, g["W_V"].T, g["W_O"].T,
                             g["router_w"].T], axis=1)
    gate = np.concatenate([g["shared_gate"].T[None], g["gate_w"]], axis=0)
    up = np.concatenate([g["shared_up"].T[None], g["up_w"]], axis=0)
    w_gu = np.concatenate([gate, up], axis=2).transpose(1, 0, 2)
    down = np.concatenate([g["shared_down"].T[None], g["down_w"]], axis=0)
    w_dn = down.reshape(9, 2, 128, 128).transpose(2, 0, 1, 3)
    pick, ones = _row_picks()
    arrays = {
        "in_x": g["x"].reshape(2048, 128), "in_w_proj": w_proj, "in_w_gu": w_gu, "in_w_dn": w_dn,
        "in_r_bias": g["routing_bias"], "in_rope": _rope_tables(), "in_pick": pick, "in_k_one": ones,
        "in_eye": np.eye(128, dtype=np.float32),
    }
    arrays = {n: np.ascontiguousarray(a) for n, a in arrays.items()}
    nc = _bacc.Bacc("TRN2", target_bir_lowering=False, num_devices=1)
    args = [nc.dram_tensor(n, a.shape, _mybir.dt.from_np(a.dtype), kind="ExternalInput").ap() for n, a in arrays.items()]
    out = nc.dram_tensor("out_0", (2048, 128), _mybir.dt.float32, kind="ExternalOutput").ap()
    w_scratch = nc.dram_tensor("w_scratch", (8, 2048), _mybir.dt.float32).ap()
    attention_moe_kernel(nc, *args, out, w_scratch)
    r = _run(nc, [arrays], core_ids=[0])
    return r.results[0]["out_0"].reshape(8, 256, 128)
```

```python
import concourse.bass as bass
from concourse import mybir
from contextlib import ExitStack


def attention_moe_kernel(nc, x, w_proj, w_gu, w_dn, r_bias, rope, pick, shapes, out, xs, ys):
    fp32 = mybir.dt.float32
    fr = mybir.dt.float32r
    i32 = mybir.dt.int32
    ALU = mybir.AluOpType
    ACT = mybir.ActivationFunctionType
    AX = mybir.AxisListType

    TOK, D = x.shape
    NE = 8
    NX = NE + 1
    BLK = 512
    NB = TOK // BLK
    T = TOK // 128
    TB = BLK // 128
    SEQ = 256
    HEADS, HD = 16, 8
    SCALE = HD ** -0.5
    EPS = 1e-5
    PV, PO = 512, 648
    VR = 128 + NE
    WP = w_proj.shape[1]
    TERMS = 3 * HD
    TERMS_MAX = TERMS + 2
    NT = 40
    BATCHES = [0, 4, 4, 2]
    assert sum(BATCHES) * 4 == NT and NT * 128 == xs.shape[0]
    PER = BATCHES[1]

    with ExitStack() as ctx:
        def sb(name, shape, dt=fp32):
            return ctx.enter_context(nc.sbuf_tensor(name, shape, dt))

        def sem(name):
            return ctx.enter_context(nc.semaphore(name))

        xr = sb("xr", [128, T, 128])
        xh = sb("xh", [128, TOK], fr)
        xl = sb("xl", [128, TOK], fr)
        wp_h = sb("wp_h", [128, WP], fr)
        wp_l = sb("wp_l", [128, WP], fr)
        gu_h = sb("gu_h", [128, NX * 512], fr)
        gu_l = sb("gu_l", [128, NX * 512], fr)
        dn = sb("dn", [128, NX * 2 * 128])
        sel = sb("sel", [128, 16, 128], fr)
        rope_t = sb("rope_t", [128, 2, BLK])
        cst = sb("cst", [128, 256 + 1 + 16 + NT])
        v_all = sb("v_all", [128, T, 128])
        v_aug = sb("v_aug", [128, TB, HEADS, 32])
        qst = sb("qst", [128, 4, BLK], fr)
        kst = sb("kst", [128, 4, BLK], fr)
        mx = sb("mx", [128, 128])
        one = sb("one", [128, 128])
        nmh = sb("nmh", [64, 128], fr)
        nml = sb("nml", [64, 128], fr)
        pt = sb("pt", [128, 2, 4, 2, 512])
        sg = sb("sg", [128, 2, 512])
        hid = sb("hid", [128, 2, 512])
        t1 = sb("t1", [128, BLK])
        t2 = sb("t2", [128, BLK])
        vh = sb("vh", [128, 2, BLK], fr)
        vl = sb("vl", [128, 2, BLK], fr)
        cx = sb("cx", [128, 4, BLK])
        cn = sb("cn", [128, TB, 128])
        ch = sb("ch", [128, BLK], fr)
        cl = sb("cl", [128, BLK], fr)
        rc = sb("rc", [128, TB, 16])
        tile_buf = sb("tile_buf", [128, 2048])
        xth = sb("xth", [128, 2, 512], fr)
        xtl = sb("xtl", [128, 2, 512], fr)
        htb = sb("htb", [128, 2, 256])
        sm = sb("sm", [128, 4, T])
        w_tok = sb("w_tok", [128, 2, T])
        pos = sb("pos", [128, 2, T], i32)
        tile_e = sb("tile_e", [1, NT], i32)
        flat = pt.rearrange("p a b c d -> p (a b c d)")
        gu_raw = flat[:, 0:NX * 512]
        sel_raw = flat[:, NX * 512:NX * 512 + 2048].rearrange("p (a n) -> p a n", a=16)
        wp_raw = flat[:, NX * 512 + 2048:NX * 512 + 2048 + WP]
        cmp_ = hid.rearrange("p a n -> p (a n)").rearrange("p (f t e) -> p f t e", f=NE, t=T)
        cmp_n = hid.rearrange("p a n -> p (a n)")[:, 0:NE * 16].rearrange("p (e j) -> p e j", e=NE)
        cmp_t = hid.rearrange("p a n -> p (a n)")[:, 128:128 + NT * NE].rearrange("p (i e) -> p i e", e=NE)
        xn = tile_buf[:, :].rearrange("p (t d) -> p t d", t=T)
        xs_t = tile_buf[:, 0:1024].rearrange("p (a j d) -> p a j d", a=2, j=4)
        sg_t = tile_buf[:, 1024:1536].rearrange("p (a n) -> p a n", a=2)
        h_t = tile_buf[:, 1536:2048].rearrange("p (a n) -> p a n", a=2)
        y_got = gu_l.bitcast(fp32)[:, 512:NX * 512].rearrange("p (s t d) -> p s t d", s=2, t=T)
        spare = cx.rearrange("p a n -> p (a n)")
        yb = spare[:, 0:1024].rearrange("p (a n) -> p a n", a=2)
        rt = spare[:, 1024:1536].rearrange("p (a n) -> p a n", a=4)
        small = spare[:, 1536:1664].rearrange("p (a n) -> p a n", a=8)
        st = spare[:, 1664:1760].rearrange("p (t k) -> p t k", t=T)
        mv = spare[:, 1760:1792].rearrange("p (t k) -> p t k", t=T)
        rbias = spare[:, 1792:1800]
        rot = [(t1[:, :], t2[:, :]), (sg[:, 0, :], sg[:, 1, :])]
        fin = cn.rearrange("p t n -> p (t n)")
        ident, tri, kone = cst[:, 0:128], cst[:, 128:256], cst[:, 256:257]
        steps, ramp = cst[:, 257:273], cst[0:1, 273:273 + NT]

        sc = ctx.enter_context(nc.psum_tensor("sc", [128, 4, 512], fp32))
        gu_p = ctx.enter_context(nc.psum_tensor("gu_p", [128, 2, 512], fp32))
        acc = ctx.enter_context(nc.psum_tensor("acc", [128, 512], fp32))
        misc = ctx.enter_context(nc.psum_tensor("misc", [128, 512], fp32))

        def sems(names):
            return [sem(n) for n in names.split()]

        ld_x = [sem(f"ld_x{j}") for j in range(4)]
        ld_gu = [sem(f"ld_gu{j}") for j in range(3)]
        ld_xs = [sem(f"ld_xs{j}") for j in range(2)]
        ld_wp, ld_c, ld_rope, ld_sel, ld_dn, ld_rb = sems("ld_wp ld_c ld_rope ld_sel ld_dn ld_rb")
        dve_chain, mx0_ok, one_ok, zero_ok, xs0 = sems("dve_chain mx0_ok one_ok zero_ok xs0")
        var_ok, sd_ok, xn_ok, xt_ok, xh_ok, xl_ok = sems("var_ok sd_ok xn_ok xt_ok xh_ok xl_ok")
        wph_ok, wpl_ok, guh_ok, gul_ok, sel_ok, vone_ok = sems("wph_ok wpl_ok guh_ok gul_ok sel_ok vone_ok")
        rt_ok, lg_ok, en_ok, mask_ok, cnt_ok, pos_ok, te_ok, sent = sems("rt_ok lg_ok en_ok mask_ok cnt_ok pos_ok te_ok sent")
        v_ok, vall_ok = sems("v_ok vall_ok")
        proj_ok, rope_ok, qk_ok, vh_ok, vl_ok = sems("proj_ok rope_ok qk_ok vh_ok vl_ok")
        pick_ok, qst_ok, kst_a, kst_d, vaug_ok = sems("pick_ok qst_ok kst_a kst_d vaug_ok")
        a_ok, mx_ok, mt_ok, nmh_ok, nml_ok = sems("a_ok mx_ok mt_ok nmh_ok nml_ok")
        mrow = [sem(f"mrow{i}") for i in range(2)]
        b_ok, ex_ok, pv_ok, cx_ok, ct_ok, rc_ok, cn_ok = sems("b_ok ex_ok pv_ok cx_ok ct_ok rc_ok cn_ok")
        cnt2_ok, ch_ok, cl_ok, f_ok, ft_ok, o_ok, st_out = sems("cnt2_ok ch_ok cl_ok f_ok ft_ok o_ok st_out")
        g_ok, u_ok, silu_ok, h_ok, down_ok = sems("g_ok u_ok silu_ok h_ok down_ok")
        tx_ok, txh_ok, txl_ok, tg_ok, ts_ok, th_ok = sems("tx_ok txh_ok txl_ok tg_ok ts_ok th_ok")
        tht_ok, tt_ok, tdn_ok, ty_ok = sems("tht_ok tt_ok tdn_ok ty_ok")
        y_st = [sem(f"y_st{j}") for j in range(2)]
        got = [sem(f"got{n}") for n in range(NB)]
        sum_ok = sem("sum_ok")

        x_v = x.rearrange("(t p) d -> p t d", p=128)
        out_v = out.rearrange("(t p) d -> p t d", p=128)
        xs_v = xs.rearrange("(i p) d -> p i d", p=128)
        ys_v = ys.rearrange("(i p) d -> p i d", p=128)

        def tok(n):
            return bass.ds(n * BLK, BLK)

        def after(eng, sem_, count):
            if not isinstance(count, int) or count > 0:
                eng.wait_ge(sem_, count)

        def pick_bank(w, hb):
            return sc[:, hb, :] if w else gu_p[:, hb % 2, :]

        def tiles(n):
            return 4 * BATCHES[n] if isinstance(n, int) else 4 * PER

        def batch0(n):
            return sum(BATCHES[:n]) if isinstance(n, int) else (n - 1) * PER

        def rows_bank(b):
            return gu_p[:, 1, :] if b == 0 else acc[:, :]

        def first_step(n):
            return 16 if tiles(n) == 0 else 3 if late(n) else 0

        def late(n):
            return isinstance(n, int) and n == NB - 1

        def shared_step(n, u):
            if late(n):
                return 16 if u == 0 else None
            return (16, 18)[u]

        def shared_banks(n, u):
            return (acc[:, :], misc[:, :]) if u == 1 and not late(n) else (gu_p[:, 0, :], gu_p[:, 1, :])

        def context_bank(n, hb):
            return misc if late(n) or hb % 2 else acc

        vr_banks = [sc[:, 0, :], sc[:, 1, :], sc[:, 2, :], sc[:, 3, :], gu_p[:, 0, :], gu_p[:, 1, :]]
        vr_tiles = [range(3 * j, min(3 * j + 3, T)) for j in range(6)]

        def vr(j, c0, c1):
            n = len(vr_tiles[j])
            return vr_banks[j][:, 0:n * VR].rearrange("p (t c) -> p t c", c=VR)[:, :, c0:c1]

        def proj_banks(n, w):
            return (acc[:, :], misc[:, :]) if w == 1 and isinstance(n, int) and n == 0 else (gu_p[:, 0, :], gu_p[:, 1, :])

        def stored(eng, it, b):
            eng.wait_ge(y_st[b % 2], (batch0(it) // 2 + b // 2 + 1) * 16 if isinstance(it, int) else (it - 1) * 8 * PER + (b // 2 + 1) * 16)

        block = ctx.enter_context(nc.Block())

        @block.sync
        def _(sp):
            for j in range(4):
                sp.dma_start(xr[:, 4 * j:4 * j + 4, :], x_v[:, 4 * j:4 * j + 4, :]).then_inc(ld_x[j], 16)
                if j == 0:
                    sp.dma_start(cst[:, :], shapes).then_inc(ld_c, 16)
            sp.dma_start(rbias[:, :], r_bias.rearrange("(a e) -> a e", a=1).to_broadcast([128, NE])).then_inc(ld_rb, 16)
            sp.dma_start(rope_t[:, :, :], rope).then_inc(ld_rope, 16)
            sp.wait_ge(ld_x[3], 16)
            for j in range(3):
                cols = slice(1536 * j, 1536 * j + 1536)
                sp.dma_start(gu_raw[:, cols], w_gu[:, cols]).then_inc(ld_gu[j], 16)
            sp.wait_ge(zero_ok, 1)
            sp.dma_start(xs_v, mx[:, :].rearrange("p (a d) -> p a d", a=1).to_broadcast([128, NT, 128])).then_inc(xs0, 16)
            sp.dma_start(dn[:, :], w_dn).then_inc(ld_dn, 16)

            def load_rows(q, b):
                sp.dma_start(xs_t[:, b % 2, :, :], xs_v[:, bass.ds(q * 4, 4), :]).then_inc(ld_xs[b % 2], 16)

            def store_rows(q, b):
                sp.wait_ge(ty_ok, q + 1)
                sp.dma_start(ys_v[:, bass.ds(q * 4, 4), :], yb[:, b % 2, :].rearrange("p (j d) -> p j d", j=4)).then_inc(y_st[b % 2], 16)

            def maxima_rows(it, half):
                sp.wait_ge(nmh_ok, it * 2 + half + 1)
                sp.wait_ge(nml_ok, it * 2 + half + 1)
                for hb in (2 * half, 2 * half + 1):
                    for k, part in enumerate((nmh, nml)):
                        sp.dma_start(qst.bitcast(fp32)[TERMS + k:TERMS + k + 97:32, hb, :],
                                     part.bitcast(fp32)[16 * hb:16 * hb + 16, :]).then_inc(mrow[half], 16)

            def body(it, last):
                n = tiles(it) // 4
                for b in range(2, n):
                    sp.wait_ge(tx_ok, batch0(it) + b - 1)
                    load_rows(batch0(it) + b, b)
                if n > 2:
                    store_rows(batch0(it), 0)
                maxima_rows(it, 0)
                for b in range(1 if n > 2 else 0, n):
                    store_rows(batch0(it) + b, b)
                maxima_rows(it, 1)
                if not last:
                    if isinstance(it, int):
                        sp.wait_ge(sent, 16 * 2 * T)
                    for b in range(2):
                        load_rows(batch0(it + 1) + b, b)

            body(0, False)
            with sp.Fori(1, NB - 1) as it:
                body(it, False)
            body(NB - 1, True)
            for n in range(NB):
                sp.wait_ge(sum_ok, n + 1)
                sp.dma_start(out_v[:, n * TB:n * TB + TB, :], xr[:, n * TB:n * TB + TB, :]).then_inc(st_out, 16)
            sp.wait_ge(st_out, 16 * NB)

        @block.gpsimd
        def _(pool):
            def rope_sum(n, w):
                pool.wait_ge(rope_ok, n * 2 + w + 1)
                pool.tensor_tensor(rot[w][0], *rot[w], ALU.add).then_inc(qk_ok, 1)

            def low_part(n, w):
                pool.wait_ge(vh_ok, n * 2 + w + 1)
                pool.tensor_tensor(vl[:, w, :], rot[w][0], vh.bitcast(fp32)[:, w, :], ALU.subtract).then_inc(vl_ok, 1)

            def values(n):
                after(pool, pv_ok, n * 4)
                pool.tensor_copy(v_aug[:, :, :, 0:HD], v_all[:, bass.ds(n * TB, TB), :].rearrange("p t (h d) -> p t h d", d=HD)).then_inc(vaug_ok, 1)

            pool.memset(mx[:, :], 0.0).then_inc(zero_ok, 1)
            pool.memset(one[:, :], 1.0).then_inc(one_ok, 1)
            pool.memset(v_aug[:, :, :, :], 1.0).then_inc(vone_ok, 1)
            pool.wait_ge(wph_ok, 1)
            pool.tensor_tensor(wp_l[:, :], wp_raw, wp_h.bitcast(fp32)[:, :], ALU.subtract).then_inc(wpl_ok, 1)

            def gate_up_low(e):
                pool.wait_ge(guh_ok, e + 1)
                cols = slice(512 * e, 512 * e + 512)
                pool.tensor_tensor(gu_l[:, cols], gu_raw[:, cols], gu_h.bitcast(fp32)[:, cols], ALU.subtract).then_inc(gul_ok, 1)

            gate_up_low(0)
            for w in range(2):
                rope_sum(0, w)
                low_part(0, w)
            for e in range(1, NX):
                gate_up_low(e)
            pool.wait_ge(vone_ok, 1)
            pool.wait_ge(vall_ok, 6)
            values(0)
            pool.wait_ge(xs0, 16)
            pool.wait_ge(pos_ok, 1)
            def send(t):
                for s in range(2):
                    pool.indirect_dma_start(out=xs, out_offset=bass.IndirectOffsetOnAxis(ap=pos[:, s, t:t + 1], axis=0),
                                            in_=xn[:, t, :], in_offset=None).then_inc(sent, 16)

            def body(it, last):
                if not last:
                    rope_sum(it + 1, 0)
                    low_part(it + 1, 0)
                    rope_sum(it + 1, 1)
                    low_part(it + 1, 1)
                    if isinstance(it, int):
                        for t in range(13, T):
                            send(t)
                    values(it + 1)

            for t in range(13):
                send(t)
            body(0, False)
            with pool.Fori(1, NB - 1) as it:
                body(it, False)
            stored(pool, NB - 1, 0)
            stored(pool, NB - 1, 1)
            for t in range(T):
                for s in range(2):
                    pool.indirect_dma_start(out=y_got[:, s, t, :], out_offset=None, in_=ys,
                                            in_offset=bass.IndirectOffsetOnAxis(ap=pos[:, s, t:t + 1], axis=0)).then_inc(got[t // TB], 16)

        @block.scalar
        def _(act):
            act.dma_start(wp_raw, w_proj).then_inc(ld_wp, 16)
            act.dma_start(sel_raw, pick).then_inc(ld_sel, 16)
            act.wait_ge(ld_wp, 16)
            act.activation(wp_h[:, :], wp_raw, ACT.Copy).then_inc(wph_ok, 1)
            act.wait_ge(ld_sel, 16)
            act.activation(sel[:, :, :], sel_raw, ACT.Copy).then_inc(sel_ok, 1)
            act.wait_ge(var_ok, 1)
            act.activation(sm[:, 1, :], sm[:, 0, :], ACT.Sqrt).then_inc(sd_ok, 1)

            def gate_up_high(e):
                act.wait_ge(ld_gu[e // 3], 16)
                cols = slice(512 * e, 512 * e + 512)
                act.activation(gu_h[:, cols], gu_raw[:, cols], ACT.Copy).then_inc(guh_ok, 1)

            for j in range(4):
                act.wait_ge(xt_ok, j + 1)
                act.activation(xh[:, tok(j)], sc[:, j, :], ACT.Copy).then_inc(xh_ok, 1)
            gate_up_high(0)
            gate_up_high(1)

            def high_part(n, w):
                act.wait_ge(qk_ok, n * 2 + w + 1)
                act.activation(vh[:, w, :], rot[w][0], ACT.Copy).then_inc(vh_ok, 1)

            def q_rows(n, hb):
                act.wait_ge(pick_ok, n * 8 + hb + 1)
                act.activation(qst[:, hb, :], pick_bank(0, hb), ACT.Copy).then_inc(qst_ok, 1)

            def k_rows(n, hb):
                act.wait_ge(pick_ok, n * 8 + 4 + hb + 1)
                act.activation(kst[:, hb, :], pick_bank(1, hb), ACT.Identity, bias=kone).then_inc(kst_a, 1)

            high_part(0, 0)
            gate_up_high(2)
            gate_up_high(3)
            high_part(0, 1)
            for j in range(6):
                act.wait_ge(lg_ok, j + 1)
                act.activation(v_all[:, 3 * j:3 * j + len(vr_tiles[j]), :], vr(j, 0, 128), ACT.Copy).then_inc(vall_ok, 1)
                if j < 5:
                    gate_up_high(4 + j)
            act.activation(rt[:, 1, :], rt[:, 0, :], ACT.Exp, scale=-1.0).then_inc(en_ok, 1)
            for hb in range(4):
                q_rows(0, hb)
            for hb in range(2):
                k_rows(0, hb)

            def tile_high(it, b):
                q = batch0(it) + b
                act.wait_ge(tx_ok, q + 1)
                if b >= 2:
                    act.wait_ge(tg_ok, (q - 1) * 4)
                act.activation(xth[:, b % 2, :], rows_bank(b), ACT.Copy).then_inc(txh_ok, 1)

            def tile_silu(it, s):
                i = batch0(it) * 4 + s
                act.wait_ge(tg_ok, i + 1)
                if s >= 2:
                    act.wait_ge(th_ok, i - 1)
                act.activation(sg_t[:, s % 2, :], gu_p[:, s % 2, 0:256], ACT.Silu).then_inc(ts_ok, 1)

            def tile_hidden_t(it, s):
                i = batch0(it) * 4 + s
                act.wait_ge(tht_ok, i + 1)
                if s >= 2:
                    act.wait_ge(tdn_ok, i - 1)
                act.activation(htb[:, s % 2, :], acc[:, 0:256], ACT.Copy).then_inc(tt_ok, 1)

            def tile_out(it, b):
                q = batch0(it) + b
                act.wait_ge(tdn_ok, q * 4 + 4)
                if b >= 2:
                    stored(act, it, b - 2)
                else:
                    act.wait_ge(ct_ok, it * 4)
                act.activation(yb[:, b % 2, :], misc[:, :], ACT.Copy).then_inc(ty_ok, 1)

            def silu(it, u):
                act.wait_ge(g_ok, it * 2 + u + 1)
                act.wait_ge(vl_ok, it * 2 + 2)
                act.activation(sg[:, u, :], shared_banks(it, u)[0], ACT.Silu).then_inc(silu_ok, 1)

            def negate_high(it, half):
                act.wait_ge(mt_ok, it * 2 + half + 1)
                after(act, mrow[half], it * 64)
                rows = slice(32 * half, 32 * half + 32)
                act.activation(nmh[rows, :], sc[rows, 2, 0:128], ACT.Copy, scale=-1.0).then_inc(nmh_ok, 1)

            def body(it, last):
                n = tiles(it)
                for s in range(18):
                    i = s - first_step(it)
                    if 0 <= i < n - 4 and i % 4 == 3:
                        tile_high(it, i // 4 + 1)
                    if 0 <= i < n:
                        tile_silu(it, i)
                    if 1 <= i <= n:
                        tile_hidden_t(it, i - 1)
                    if 5 <= i <= n + 1 and i % 4 == 1:
                        tile_out(it, (i - 5) // 4)
                    if s == 8:
                        negate_high(it, 0)
                    if s == shared_step(it, 0):
                        silu(it, 0)
                    if s == shared_step(it, 1):
                        silu(it, 1)
                negate_high(it, 1)
                if shared_step(it, 1) == 18:
                    silu(it, 1)
                if isinstance(it, int) and it == 0:
                    act.wait_ge(gul_ok, NX)
                for p in range(16):
                    hb, g = p // 4, p % 4
                    act.wait_ge(b_ok, it * 16 + p + 1)
                    after(act, pv_ok, it * 4 + max(hb - 1, 0))
                    act.activation(pt[:, hb % 2, g, :, :], sc[:, 2 * (p % 2):2 * (p % 2) + 2, :], ACT.Exp, scale=SCALE).then_inc(ex_ok, 1)
                if last:
                    silu(it, 1)
                else:
                    for hb in range(4):
                        q_rows(it + 1, hb)
                    tile_high(it + 1, 0)
                act.wait_ge(cnt2_ok, it + 1)
                act.activation(ch[:, :], misc[:, :], ACT.Copy).then_inc(ch_ok, 1)
                if not last:
                    for hb in range(2):
                        k_rows(it + 1, hb)
                act.wait_ge(down_ok, it + 1)
                after(act, ft_ok, it)
                act.activation(fin, acc[:, :], ACT.Copy).then_inc(f_ok, 1)

            body(0, False)
            with act.Fori(1, NB - 1) as it:
                body(it, False)
            body(NB - 1, True)

        @block.vector
        def _(dve):
            chain = [0]

            def link(ins):
                chain[0] += 1
                ins.then_inc(dve_chain, 1)
                dve.wait_ge(dve_chain, chain[0])

            for t in range(T):
                dve.wait_ge(ld_x[t // 4], 16)
                last_st = dve.bn_stats(st[:, t, :], xr[:, t, :])
            link(last_st)
            for t in range(T):
                last_mv = dve.bn_aggr(mv[:, t, :], st[:, t, :])
            link(last_mv)
            dve.tensor_scalar(sm[:, 0, :], mv[:, :, 1], EPS, None, ALU.add).then_inc(var_ok, 1)
            dve.wait_ge(sd_ok, 1)
            link(dve.reciprocal(sm[:, 2, :], sm[:, 1, :]))
            link(dve.tensor_tensor(sm[:, 1, :], sm[:, 2, :], sm[:, 2, :], ALU.mult))
            link(dve.tensor_tensor(sm[:, 3, :], sm[:, 1, :], sm[:, 0, :], ALU.mult))
            link(dve.tensor_scalar(sm[:, 1, :], sm[:, 3, :], -0.5, 1.5, ALU.mult, ALU.add))
            link(dve.tensor_tensor(sm[:, 3, :], sm[:, 1, :], sm[:, 2, :], ALU.mult))
            for t in range(T):
                dve.tensor_scalar(xn[:, t, :], xr[:, t, :], mv[:, t, 0:1], sm[:, 3, t:t + 1], ALU.subtract, ALU.mult).then_inc(xn_ok, 1)
            for j in range(4):
                dve.wait_ge(xh_ok, j + 1)
                dve.tensor_tensor(xl[:, tok(j)], sc[:, j, :], xh.bitcast(fp32)[:, tok(j)], ALU.subtract).then_inc(xl_ok, 1)

            def rotate(n, w):
                dve.wait_ge(proj_ok, n * 2 + w + 1)
                if w == 0:
                    after(dve, vl_ok, n * 2)
                elif not (isinstance(n, int) and n == 0):
                    dve.wait_ge(h_ok, n * 2)
                plain, swapped = proj_banks(n, w)
                dve.tensor_tensor(rot[w][0], plain, rope_t[:, 0, :], ALU.mult)
                dve.tensor_tensor(rot[w][1], swapped, rope_t[:, 1, :], ALU.mult).then_inc(rope_ok, 1)

            def high_part(n, w):
                dve.wait_ge(qk_ok, n * 2 + w + 1)
                dve.wait_ge(pick_ok, n * 8)
                dve.tensor_copy(vh[:, w, :], rot[w][0]).then_inc(vh_ok, 1)

            def k_rows(n, hb):
                dve.wait_ge(pick_ok, n * 8 + 4 + hb + 1)
                dve.tensor_scalar(kst[:, hb, :], pick_bank(1, hb), kone, None, ALU.add).then_inc(kst_d, 1)

            te = lambda a: a.rearrange("p (t e) -> p t e", t=T)
            et = lambda a: a.rearrange("p (e t) -> p e t", e=NE)
            per_t = lambda a: a.rearrange("p e t -> p t e")

            dve.wait_ge(ld_rope, 16)
            rotate(0, 0)
            rotate(0, 1)
            dve.wait_ge(ld_rb, 16)
            for j, tt in enumerate(vr_tiles):
                dve.wait_ge(v_ok, j + 1)
                bias_b = rbias[:, :].rearrange("p (a e) -> p a e", a=1).to_broadcast([128, len(tt), NE])
                dve.tensor_tensor(te(rt[:, 0, :])[:, tt[0]:tt[0] + len(tt), :], vr(j, 128, VR), bias_b, ALU.add).then_inc(lg_ok, 1)
            dve.wait_ge(en_ok, 1)
            link(dve.tensor_scalar(rt[:, 2, :], rt[:, 1, :], 1.0, None, ALU.add))
            link(dve.reciprocal(rt[:, 3, :], rt[:, 2, :]))
            prob = te(rt[:, 3, :])
            for f in range(NE):
                own = prob[:, :, f:f + 1]
                if f > 0:
                    last_c = dve.tensor_tensor(cmp_[:, f, :, 0:f], own.to_broadcast([128, T, f]), prob[:, :, 0:f], ALU.is_gt)
                last_c = dve.tensor_tensor(cmp_[:, f, :, f:NE], own.to_broadcast([128, T, NE - f]), prob[:, :, f:NE], ALU.is_ge)
            link(last_c)
            link(dve.tensor_reduce(te(rt[:, 0, :]), cmp_.rearrange("p f t e -> p t e f"), AX.X, ALU.add))
            dve.tensor_scalar(per_t(et(rt[:, 1, :])), te(rt[:, 0, :]), 2.5, None, ALU.is_lt).then_inc(mask_ok, 1)
            for hb in (2, 3):
                k_rows(0, hb)
            dve.wait_ge(mask_ok, 1)
            link(dve.tensor_tensor(per_t(et(rt[:, 2, :])), per_t(et(rt[:, 1, :])), prob, ALU.mult))
            link(dve.tensor_reduce(small[:, 0, :], per_t(et(rt[:, 2, :])), AX.X, ALU.add))
            link(dve.reciprocal(small[:, 1, :], small[:, 0, :]))
            share = small[:, 1, :].rearrange("p (a t) -> p a t", a=1).to_broadcast([128, NE, T])
            link(dve.tensor_tensor(et(rt[:, 2, :]), et(rt[:, 2, :]), share, ALU.mult))
            dve.wait_ge(cnt_ok, 1)
            counts, upto, place = rt[:, 3, :], rt[:, 0, :], hid.rearrange("p a n -> p (a n)")
            link(dve.tensor_copy(counts, misc[:, 128:256]))
            link(dve.tensor_tensor_scan(upto, one[:, :], counts, 0.0, ALU.mult, ALU.add))
            n_e, nt_e, end_e, base_e = (small[:, 2 + k, 0:NE] for k in range(4))
            link(dve.tensor_reduce(n_e, et(counts), AX.X, ALU.add))
            over = n_e.rearrange("p (e a) -> p e a", a=1).to_broadcast([128, NE, 16])
            limit = steps.rearrange("p (a j) -> p a j", a=1).to_broadcast([128, NE, 16])
            link(dve.tensor_tensor(cmp_n, over, limit, ALU.is_gt))
            link(dve.tensor_reduce(nt_e, cmp_n, AX.X, ALU.add))
            link(dve.tensor_tensor_scan(end_e, one[:, 0:NE], nt_e, 0.0, ALU.mult, ALU.add))
            ends = end_e[0:1].rearrange("p (a e) -> p a e", a=1).to_broadcast([1, NT, NE])
            link(dve.tensor_tensor(cmp_t[0:1], ends, ramp.rearrange("p (i a) -> p i a", a=1).to_broadcast([1, NT, NE]), ALU.is_le))
            link(dve.tensor_reduce(place[0:1, 512:512 + NT], cmp_t[0:1], AX.X, ALU.add))
            dve.tensor_scalar(tile_e[:, :], place[0:1, 512:512 + NT], float(NE - 1), 1.0, ALU.min, ALU.add).then_inc(te_ok, 1)
            link(dve.tensor_tensor(base_e, end_e, nt_e, ALU.subtract))
            link(dve.scalar_tensor_tensor(out=base_e, in0=base_e, scalar=128.0, in1=n_e, op0=ALU.mult, op1=ALU.add))
            link(dve.tensor_tensor(base_e, base_e, et(upto)[:, :, T - 1], ALU.subtract))
            link(dve.tensor_tensor(upto, upto, counts, ALU.subtract))
            link(dve.tensor_tensor(upto, misc[:, 0:128], upto, ALU.add))
            link(dve.tensor_tensor(et(upto), et(upto), base_e.rearrange("p (e a) -> p e a", a=1).to_broadcast([128, NE, T]), ALU.add))
            link(dve.tensor_tensor(upto, upto, rt[:, 1, :], ALU.mult))
            link(dve.tensor_reduce(small[:, 6, :], per_t(et(upto)), AX.X, ALU.max))
            link(dve.tensor_reduce(small[:, 7, :], per_t(et(upto)), AX.X, ALU.add))
            dve.tensor_copy(pos[:, 1, :], small[:, 6, :])
            dve.tensor_tensor(pos[:, 0, :], small[:, 7, :], small[:, 6, :], ALU.subtract).then_inc(pos_ok, 1)

            def token_weights():
                later = small[:, 6, :].rearrange("p (a t) -> p a t", a=1).to_broadcast([128, NE, T])
                for s, op in enumerate((ALU.is_lt, ALU.is_ge)):
                    link(dve.tensor_tensor(et(counts), et(upto), later, op))
                    link(dve.tensor_tensor(counts, counts, rt[:, 2, :], ALU.mult))
                    link(dve.tensor_reduce(w_tok[:, s, :], per_t(et(counts)), AX.X, ALU.add))

            token_weights()

            def tile_low(it, b):
                dve.wait_ge(txh_ok, batch0(it) + b + 1)
                dve.tensor_tensor(xtl[:, b % 2, :], rows_bank(b), xth.bitcast(fp32)[:, b % 2, :], ALU.subtract).then_inc(txl_ok, 1)

            def tile_hidden(it, s):
                i = batch0(it) * 4 + s
                dve.wait_ge(ts_ok, i + 1)
                if s >= 2:
                    dve.wait_ge(tht_ok, i - 1)
                dve.tensor_tensor(h_t[:, s % 2, :], gu_p[:, s % 2, 256:512], sg_t[:, s % 2, :], ALU.mult).then_inc(th_ok, 1)

            def hidden(it, u):
                dve.wait_ge(silu_ok, it * 2 + u + 1)
                dve.wait_ge(u_ok, it * 2 + u + 1)
                dve.tensor_tensor(hid[:, u, :], shared_banks(it, u)[1], sg[:, u, :], ALU.mult).then_inc(h_ok, 1)

            def maxima(it, a):
                dve.wait_ge(a_ok, it * 16 + a + 1)
                dve.tensor_reduce(mx[:, 4 * a:4 * a + 4], sc[:, 2 * (a % 2):2 * (a % 2) + 2, :].rearrange("p b (q k) -> p (b q) k", q=2),
                                  AX.X, ALU.max).then_inc(mx_ok, 1)

            def negate_low(it, half):
                dve.wait_ge(nmh_ok, it * 2 + half + 1)
                rows = slice(32 * half, 32 * half + 32)
                dve.scalar_tensor_tensor(out=nml[rows, :], in0=sc[rows, 2, 0:128], scalar=-1.0, in1=nmh.bitcast(fp32)[rows, :],
                                         op0=ALU.mult, op1=ALU.subtract).then_inc(nml_ok, 1)

            def finish(it):
                dve.wait_ge(ft_ok, it + 1)
                mine = xr[:, bass.ds(it * TB, TB), :]
                dve.tensor_tensor(mine, misc[:, :].rearrange("p (t d) -> p t d", t=TB), mine, ALU.add).then_inc(o_ok, 1)

            def body(it, last):
                n = tiles(it)
                for s in range(16):
                    i = s - first_step(it)
                    if 0 <= i < n - 4 and i % 4 == 3:
                        tile_low(it, i // 4 + 1)
                    if 0 <= i < n:
                        tile_hidden(it, i)
                    if s == 0:
                        if isinstance(it, int) and it == 0:
                            dve.wait_ge(xs0, 16)
                        after(dve, mt_ok, it * 2)
                    if s == 8:
                        dve.wait_ge(mt_ok, it * 2 + 1)
                    maxima(it, s)
                    if s == 8:
                        negate_low(it, 0)
                    if s == 0 and n:
                        finish(it - 1)
                negate_low(it, 1)
                hidden(it, 0)
                if not last:
                    hidden(it, 1)
                    rotate(it + 1, 0)
                    high_part(it + 1, 0)
                    rotate(it + 1, 1)
                    high_part(it + 1, 1)
                if n:
                    stored(dve, it, n // 4 - 2)
                    stored(dve, it, n // 4 - 1)
                for hb in range(4):
                    dve.wait_ge(pv_ok, it * 4 + hb + 1)
                    after(dve, ct_ok, it * 4)
                    dve.tensor_copy(cx[:, hb, :], context_bank(it, hb)[:, :]).then_inc(cx_ok, 1)
                    if last and hb >= 2:
                        combine(hb - 2)
                if last:
                    hidden(it, 1)
                after(dve, ft_ok, it)
                for t in range(TB):
                    dve.wait_ge(ct_ok, it * 4 + t + 1)
                    by_head = sc[:, t, :].rearrange("p (b g c) -> p b g c", g=4, c=32)
                    dve.reciprocal(rc[:, t, :].rearrange("p (b g) -> p b g", g=4), by_head[:, :, :, HD]).then_inc(rc_ok, 1)
                    dve.wait_ge(rc_ok, it * 4 + t + 1)
                    dve.tensor_tensor(cn[:, t, :].rearrange("p (g b d) -> p b g d", g=4, b=4), by_head[:, :, :, 0:HD],
                                      rc[:, t, :].rearrange("p (b g a) -> p b g a", g=4, a=1).to_broadcast([128, 4, 4, HD]),
                                      ALU.mult).then_inc(cn_ok, 1)
                if not last:
                    tile_low(it + 1, 0)
                dve.wait_ge(ch_ok, it + 1)
                dve.tensor_tensor(cl[:, :], misc[:, :], ch.bitcast(fp32)[:, :], ALU.subtract).then_inc(cl_ok, 1)
                if last:
                    combine(NB - 2)
                else:
                    for hb in (2, 3):
                        k_rows(it + 1, hb)

            def combine(n):
                dve.wait_ge(got[n], 16 * 2 * TB)
                dve.wait_ge(o_ok, n + 1)
                for s in range(2):
                    for t in range(n * TB, n * TB + TB):
                        last_s = dve.scalar_tensor_tensor(out=xr[:, t, :], in0=y_got[:, s, t, :], scalar=w_tok[:, s, t:t + 1],
                                                          in1=xr[:, t, :], op0=ALU.mult, op1=ALU.add)
                    if s == 0:
                        link(last_s)
                last_s.then_inc(sum_ok, 1)

            body(0, False)
            with dve.Fori(1, NB - 1) as it:
                body(it, False)
            body(NB - 1, True)
            finish(NB - 1)
            combine(NB - 1)

        @block.tensor
        def _(pe):
            def three(dst, lhs_h, lhs_l, rhs_h, rhs_l, start=True, stop=True):
                pe.matmul(dst, lhs_h, rhs_h, start=start, stop=False)
                pe.matmul(dst, lhs_h, rhs_l, start=False, stop=False)
                return pe.matmul(dst, lhs_l, rhs_h, start=False, stop=stop)

            def wp(c, n=128):
                return wp_h[:, c:c + n], wp_l[:, c:c + n]

            def project(n, w):
                for s, bank in enumerate(proj_banks(n, w)):
                    last = three(bank, *wp((2 * w + s) * 128), xh[:, tok(n)], xl[:, tok(n)])
                last.then_inc(proj_ok, 1)

            def pick_rows(n, w, hb):
                pe.wait_ge(vl_ok, n * 2 + w + 1)
                first = isinstance(n, int) and n == 0
                if w == 0 and hb < 2 and first:
                    pe.wait_ge(vall_ok, 5 + hb)
                elif w == 0 and hb < 2:
                    pe.wait_ge(rope_ok, n * 2 + 2)
                elif w == 0:
                    pe.wait_ge(qst_ok, n * 4 + hb - 1)
                elif first:
                    pe.wait_ge(vall_ok, hb + 1)
                else:
                    pe.wait_ge(cn_ok, (n - 1) * 4 + hb + 1)
                dst = pick_bank(w, hb)
                pe.matmul(dst, sel[:, 8 * w + hb, :], vh[:, w, :], start=True, stop=False)
                pe.matmul(dst, sel[:, 8 * w + 4 + hb, :], vl[:, w, :], start=False, stop=True).then_inc(pick_ok, 1)

            pe.wait_ge(ld_c, 16)
            for j in range(4):
                for t in range(4 * j, 4 * j + 4):
                    pe.wait_ge(xn_ok, t + 1)
                    last = pe.transpose(sc[:, j, (t % 4) * 128:(t % 4) * 128 + 128], xn[:, t, :], ident)
                last.then_inc(xt_ok, 1)
            pe.wait_ge(wpl_ok, 1)
            pe.wait_ge(xl_ok, 1)
            project(0, 0)
            project(0, 1)
            for j, tt in enumerate(vr_tiles):
                if j < 4:
                    pe.wait_ge(xl_ok, 4)
                else:
                    pe.wait_ge(rope_ok, 1)
                for k, t in enumerate(tt):
                    cols = slice(128 * t, 128 * t + 128)
                    last = three(vr_banks[j][:, k * VR:k * VR + VR], xh[:, cols], xl[:, cols], *wp(PV, VR))
                last.then_inc(v_ok, 1)
            pe.wait_ge(sel_ok, 1)
            for w in range(2):
                for hb in range(4):
                    pick_rows(0, w, hb)
            pe.wait_ge(mask_ok, 1)
            pe.wait_ge(one_ok, 1)
            pe.matmul(misc[:, 0:128], tri, rt[:, 1, :], start=True, stop=True)
            pe.matmul(misc[:, 128:256], one[:, :], rt[:, 1, :], start=True, stop=True).then_inc(cnt_ok, 1)

            def gate_up(it, u):
                gate, up = shared_banks(it, u)
                if u == 0 and tiles(it):
                    pe.wait_ge(th_ok, batch0(it) * 4 + tiles(it))
                elif u == 1 and late(it):
                    pe.wait_ge(h_ok, it * 2 + 1)
                elif u == 1 and tiles(it):
                    pe.wait_ge(tt_ok, batch0(it) * 4 + tiles(it))
                three(gate, gu_h[:, u * 128:u * 128 + 128], gu_l[:, u * 128:u * 128 + 128],
                      xh[:, tok(it)], xl[:, tok(it)]).then_inc(g_ok, 1)
                if u == 1 and not late(it):
                    if tiles(it):
                        pe.wait_ge(ty_ok, batch0(it) + tiles(it) // 4)
                    else:
                        pe.wait_ge(pos_ok, 1)
                o = 256 + u * 128
                three(up, gu_h[:, o:o + 128], gu_l[:, o:o + 128],
                      xh[:, tok(it)], xl[:, tok(it)]).then_inc(u_ok, 1)

            def down(it, u):
                pe.wait_ge(h_ok, it * 2 + u + 1)
                pe.matmul(acc[:, :], dn[:, u * 128:u * 128 + 128], hid[:, u, :], start=(u == 0), stop=False)

            def tile_rows(it, b):
                q = batch0(it) + b
                pe.wait_ge(ld_xs[b % 2], (q // 2 + 1) * 16 if isinstance(it, int) else (it - 1) * 8 * PER + (b // 2 + 1) * 16)
                if b == 0:
                    pe.wait_ge(qst_ok, it * 4 + 4)
                else:
                    pe.wait_ge(tt_ok, batch0(it) * 4 + 4 * b - 2)
                for j in range(4):
                    last = pe.transpose(rows_bank(b)[:, j * 128:j * 128 + 128], xs_t[:, b % 2, j, :], ident)
                last.then_inc(tx_ok, 1)

            def expert(it, s):
                return pe.value_load(tile_e[0:1, bass.ds(batch0(it) * 4 + s, 1)], min_val=1, max_val=NE)

            experts = {}

            def tile_gate_up(it, s):
                i, b, j = batch0(it) * 4 + s, s // 4, s % 4
                if s == 0:
                    experts[0] = expert(it, 0)
                e = experts[s]
                if j == 0:
                    pe.wait_ge(txl_ok, batch0(it) + b + 1)
                if s < 2:
                    pe.wait_ge(txl_ok, batch0(it) + 1)
                else:
                    pe.wait_ge(th_ok, i - 1)
                cols = bass.ds(e * 512, 512)
                three(gu_p[:, s % 2, :], xth[:, b % 2, j * 128:j * 128 + 128], xtl[:, b % 2, j * 128:j * 128 + 128],
                      gu_h[:, cols], gu_l[:, cols]).then_inc(tg_ok, 1)
                if s + 1 < tiles(it):
                    experts[s + 1] = expert(it, s + 1)

            def tile_turn(it, s):
                i = batch0(it) * 4 + s
                pe.wait_ge(th_ok, i + 1)
                if s == 0:
                    pe.wait_ge(f_ok, it)
                elif s % 4 == 2 and s // 4 + 1 < tiles(it) // 4:
                    pe.wait_ge(txl_ok, batch0(it) + (s + 2) // 4 + 1)
                else:
                    pe.wait_ge(tt_ok, i)
                for c in range(2):
                    last = pe.transpose(acc[:, c * 128:c * 128 + 128], h_t[:, s % 2, c * 128:c * 128 + 128], ident)
                last.then_inc(tht_ok, 1)

            def tile_down(it, s):
                i, b, j = batch0(it) * 4 + s, s // 4, s % 4
                e = experts[s]
                pe.wait_ge(tt_ok, i + 1)
                if s == 0:
                    pe.wait_ge(o_ok, it)
                elif j == 0:
                    pe.wait_ge(ty_ok, batch0(it) + b)
                for c in range(2):
                    last = pe.matmul(misc[:, j * 128:j * 128 + 128], htb[:, s % 2, c * 128:c * 128 + 128],
                                     dn[:, bass.ds(e * 256 + c * 128, 128)], start=(c == 0), stop=(c == 1))
                last.then_inc(tdn_ok, 1)

            def scores(it, a):
                g, hb = a % 4, a // 4
                if a == 0:
                    pe.wait_ge(qst_ok, it * 4 + 4)
                    pe.wait_ge(kst_a, it * 2 + 2)
                if a == 1:
                    pe.wait_ge(kst_d, it * 2 + 2)
                if a == 9:
                    pe.wait_ge(nml_ok, it * 2 + 1)
                if a >= 2:
                    pe.wait_ge(mx_ok, it * 16 + a - 1)
                rows = slice(32 * g, 32 * g + TERMS)
                for b in range(2):
                    for qt in range(2):
                        q0 = b * SEQ + qt * 128
                        last = pe.matmul(sc[:, 2 * (a % 2) + b, qt * SEQ:qt * SEQ + SEQ], qst[rows, hb, q0:q0 + 128],
                                         kst[rows, hb, b * SEQ:b * SEQ + SEQ], start=True, stop=True)
                last.then_inc(a_ok, 1)

            def scores_t(it, p):
                hb, g = p // 4, p % 4
                if p % 8 == 0:
                    pe.wait_ge(mrow[p // 8], it * 64 + 64)
                if p == 0:
                    pe.wait_ge(mx_ok, it * 16 + 16)
                if p == 1:
                    pe.wait_ge(nml_ok, it * 2 + 2)
                if p >= 2:
                    pe.wait_ge(ex_ok, it * 16 + p - 1)
                rows = slice(32 * g, 32 * g + TERMS_MAX)
                for b in range(2):
                    for kt in range(2):
                        k0 = b * SEQ + kt * 128
                        last = pe.matmul(sc[:, 2 * (p % 2) + b, kt * SEQ:kt * SEQ + SEQ], kst[rows, hb, k0:k0 + 128],
                                         qst[rows, hb, b * SEQ:b * SEQ + SEQ], start=True, stop=True)
                last.then_inc(b_ok, 1)

            def context(it, hb, b, kt):
                bank = context_bank(it, hb)
                if (b, kt) == (0, 0):
                    pe.wait_ge(ex_ok, it * 16 + 4 * hb + 4)
                    context_start(it, hb)
                for g in range(4):
                    last = pe.matmul(bank[32 * g:32 * g + 32, b * SEQ:b * SEQ + SEQ], v_aug[:, 2 * b + kt, 4 * g + hb, :],
                                     pt[:, hb % 2, g, b, kt * SEQ:kt * SEQ + SEQ], start=(kt == 0), stop=(kt == 1))
                if (b, kt) == (1, 1):
                    last.then_inc(pv_ok, 1)

            def context_start(it, hb):
                if hb == 0:
                    pe.wait_ge(vaug_ok, it + 1)
                    if not late(it):
                        pe.wait_ge(silu_ok, it * 2 + 2)
                elif late(it):
                    pe.wait_ge(cx_ok, it * 4 + hb)
                elif hb == 1:
                    pe.wait_ge(h_ok, it * 2 + 2)
                else:
                    pe.wait_ge(cx_ok, it * 4 + hb - 1)

            def turn_maxima(it, half):
                pe.wait_ge(mx_ok, it * 16 + 8 * half + 8)
                pe.transpose(sc[:, 2, 0:128], mx[:, :], ident).then_inc(mt_ok, 1)

            def finish(it):
                pe.wait_ge(f_ok, it + 1)
                for t in range(TB):
                    last = pe.transpose(misc[:, t * 128:t * 128 + 128], fin[:, t * 128:t * 128 + 128], ident)
                last.then_inc(ft_ok, 1)

            def body(it, last_block):
                n = tiles(it)
                for s in range(18):
                    i = s - first_step(it)
                    if 0 <= i < n - 4 and i % 4 == 3:
                        tile_rows(it, i // 4 + 1)
                    if 0 <= i < n:
                        tile_gate_up(it, i)
                    if s < 16:
                        scores(it, s)
                    if s == 0 and n:
                        finish(it - 1)
                    if s == 8:
                        turn_maxima(it, 0)
                    if 1 <= i <= n:
                        tile_turn(it, i - 1)
                    if 2 <= i <= n + 1:
                        tile_down(it, i - 2)
                    if s == shared_step(it, 0) and isinstance(it, int) and it == 0:
                        pe.wait_ge(ld_dn, 16)
                        pe.wait_ge(gul_ok, NX)
                        pe.wait_ge(te_ok, 1)
                        pe.wait_ge(pos_ok, 1)
                    if s == shared_step(it, 0):
                        gate_up(it, 0)
                    if s == shared_step(it, 1):
                        gate_up(it, 1)
                turn_maxima(it, 1)
                if shared_step(it, 1) == 18:
                    gate_up(it, 1)
                for p in range(16):
                    scores_t(it, p)
                    if p == 1:
                        if last_block:
                            gate_up(it, 1)
                        else:
                            pe.wait_ge(h_ok, it * 2 + 1)
                            project(it + 1, 0)
                    if p == 3:
                        if last_block:
                            down(it, 0)
                        else:
                            pe.wait_ge(rope_ok, (it + 1) * 2 + 1)
                            project(it + 1, 1)
                    if p >= 4:
                        context(it, p // 4 - 1, p // 2 % 2, p % 2)
                if not last_block:
                    pick_rows(it + 1, 0, 0)
                    pick_rows(it + 1, 0, 1)
                for b in range(2):
                    for kt in range(2):
                        context(it, 3, b, kt)
                if not last_block:
                    pick_rows(it + 1, 0, 2)
                pe.wait_ge(cx_ok, it * 4 + 4)
                for t in range(TB):
                    for hb in range(4):
                        last = pe.transpose(sc[:, t, hb * 128:hb * 128 + 128], cx[:, hb, t * 128:t * 128 + 128], ident)
                    last.then_inc(ct_ok, 1)
                if not last_block:
                    pick_rows(it + 1, 0, 3)
                for t in range(TB):
                    pe.wait_ge(cn_ok, it * 4 + t + 1)
                    last = pe.transpose(misc[:, t * 128:t * 128 + 128], cn[:, t, :], ident)
                last.then_inc(cnt2_ok, 1)
                if last_block:
                    down(it, 1)
                else:
                    tile_rows(it + 1, 0)
                    for hb in range(4):
                        pick_rows(it + 1, 1, hb)
                    down(it, 0)
                    down(it, 1)
                pe.wait_ge(cl_ok, it + 1)
                three(acc[:, :], *wp(PO), ch[:, :], cl[:, :], start=False).then_inc(down_ok, 1)

            body(0, False)
            with pe.Fori(1, NB - 1) as it:
                body(it, False)
            body(NB - 1, True)
            finish(NB - 1)


def _rope_tables():
    import numpy as np
    hd, seq = 8, 256
    inv = (1.0 / np.float32(10000.0) ** (np.arange(0, hd, 2, dtype=np.float32) / np.float32(hd))).astype(np.float32)
    ang = np.outer(np.arange(seq, dtype=np.float32), inv).astype(np.float32)
    cos, sin = np.cos(ang), np.sin(ang)
    table = np.zeros((128, 2, 512), np.float32)
    for e in range(128):
        i = (e % hd) // 2
        table[e, 0] = np.tile(cos[:, i], 2)
        table[e, 1] = np.tile(sin[:, i], 2) * (1.0 if e % 2 else -1.0)
    return table


def _row_picks():
    import numpy as np
    pick = np.zeros((128, 4, 4, 128), np.float32)
    parts = [(0, 1), (2,), (0, 2), (1,)]
    for kind, terms in enumerate(parts):
        for hb in range(4):
            for g in range(4):
                for d in range(8):
                    for j in terms:
                        pick[8 * (4 * g + hb) + d, kind, hb, 32 * g + 8 * j + d] = 1.0
    ones = np.zeros((128, 1), np.float32)
    for g in range(4):
        ones[32 * g + 24:32 * g + 26] = 1.0
    return pick.reshape(128, 16, 128), ones


def kernel(**inputs):
    import numpy as np
    import concourse.bacc as _bacc
    from concourse import mybir as _mybir
    from concourse.bass_utils import run_bass_kernel_spmd as _run

    g = {k.replace("L0_attn_", "").replace("L0_ffn_", ""): np.asarray(v) for k, v in inputs.items()}
    swap = np.arange(128).reshape(64, 2)[:, ::-1].reshape(-1)
    w_proj = np.concatenate([g["W_Q"].T, g["W_Q"][swap].T, g["W_K"].T, g["W_K"][swap].T, g["W_V"].T,
                             g["router_w"].T, g["W_O"].T], axis=1)
    gate = np.concatenate([g["shared_gate"].T[None], g["gate_w"]], axis=0)
    up = np.concatenate([g["shared_up"].T[None], g["up_w"]], axis=0)
    w_gu = np.concatenate([gate, up], axis=2).transpose(1, 0, 2).reshape(128, -1)
    down = np.concatenate([g["shared_down"].T[None], g["down_w"]], axis=0)
    w_dn = down.reshape(9, 2, 128, 128).transpose(2, 0, 1, 3).reshape(128, -1)
    pick, ones = _row_picks()
    arrays = {
        "in_x": g["x"].reshape(2048, 128), "in_w_proj": w_proj, "in_w_gu": w_gu, "in_w_dn": w_dn,
        "in_r_bias": g["routing_bias"], "in_rope": _rope_tables(), "in_pick": pick,
        "in_shapes": np.concatenate([np.eye(128), np.triu(np.ones((128, 128)), 1), ones,
                                     np.tile(128.0 * np.arange(16), (128, 1)),
                                     np.tile(np.arange(40.0), (128, 1))], axis=1).astype(np.float32),
    }
    arrays = {n: np.ascontiguousarray(a) for n, a in arrays.items()}
    nc = _bacc.Bacc("TRN2", target_bir_lowering=False, num_devices=1)
    args = [nc.dram_tensor(n, a.shape, _mybir.dt.from_np(a.dtype), kind="ExternalInput").ap() for n, a in arrays.items()]
    out = nc.dram_tensor("out_0", (2048, 128), _mybir.dt.float32, kind="ExternalOutput").ap()
    xs, ys = (nc.dram_tensor(n, (40 * 128, 128), _mybir.dt.float32).ap() for n in ("sorted_rows", "sorted_results"))
    attention_moe_kernel(nc, *args, out, xs, ys)
    r = _run(nc, [arrays], core_ids=[0])
    return r.results[0]["out_0"].reshape(8, 256, 128)
```

```python
import concourse.bass as bass
from concourse import mybir
from contextlib import ExitStack


def attention_moe_kernel(nc, x, w_proj, w_gu, w_dn, r_bias, rope, shapes, out, xs, ys):
    fp32 = mybir.dt.float32
    fr = mybir.dt.float32r
    i32 = mybir.dt.int32
    ALU = mybir.AluOpType
    ACT = mybir.ActivationFunctionType
    AX = mybir.AxisListType

    TOK, D = x.shape
    NE = 8
    NX = NE + 1
    BLK = 512
    NB = TOK // BLK
    T = TOK // 128
    TB = BLK // 128
    SEQ = 256
    HEADS, HD = 16, 8
    SCALE = HD ** -0.5
    EPS = 1e-5
    PV, PO = 512, 648
    VR = 128 + NE
    WP = w_proj.shape[1]
    ROW_STEP = 4
    MAX_HIGH, MAX_LOW = 3, 7
    LAID = 7 * 16
    NT = 40
    BATCHES = [0, 4, 4, 2]
    STEPS = HEADS
    LAST_STEPS = [0, 1, 2, 3, 5, 6, 8, 9]
    assert sum(BATCHES) * 4 == NT and NT * 128 == xs.shape[0]
    PER = BATCHES[1]

    with ExitStack() as ctx:
        def sb(name, shape, dt=fp32):
            return ctx.enter_context(nc.sbuf_tensor(name, shape, dt))

        def sem(name):
            return ctx.enter_context(nc.semaphore(name))

        xr = sb("xr", [128, T, 128])
        xh = sb("xh", [128, TOK], fr)
        xl = sb("xl", [128, TOK], fr)
        wp_h = sb("wp_h", [128, WP], fr)
        wp_l = sb("wp_l", [128, WP], fr)
        gu_h = sb("gu_h", [128, NX * 512], fr)
        gu_l = sb("gu_l", [128, NX * 512], fr)
        dn = sb("dn", [128, NX * 2 * 128])
        rope_t = sb("rope_t", [128, 2, BLK])
        cst = sb("cst", [128, 256 + 16 + NT])
        v_all = sb("v_all", [128, T, 128])
        v_aug = sb("v_aug", [128, TB, HEADS, 32])
        qst = sb("qst", [128, 4, BLK], fr)
        kst = sb("kst", [128, 4, BLK], fr)
        nil = sb("nil", [32, BLK])
        mx = sb("mx", [128, 128])
        one = sb("one", [128, 128])
        nmh = sb("nmh", [64, 128], fr)
        nml = sb("nml", [64, 128], fr)
        pt = sb("pt", [128, 2, 4, 2, 512])
        sg = sb("sg", [128, 2, 512])
        hid = sb("hid", [128, 2, 512])
        t1 = sb("t1", [128, BLK])
        t2 = sb("t2", [128, BLK])
        vh = sb("vh", [128, 2, BLK], fr)
        vl = sb("vl", [128, 2, BLK], fr)
        cx = sb("cx", [128, 4, BLK])
        cn = sb("cn", [128, TB, 128])
        ch = sb("ch", [128, BLK], fr)
        cl = sb("cl", [128, BLK], fr)
        rc = sb("rc", [128, TB, 16])
        tile_buf = sb("tile_buf", [128, 2048])
        xth = sb("xth", [128, 2, 512], fr)
        xtl = sb("xtl", [128, 2, 512], fr)
        htb = sb("htb", [128, 2, 256])
        sm = sb("sm", [128, 4, T])
        w_tok = sb("w_tok", [128, 2, T])
        pos = sb("pos", [128, 2, T], i32)
        tile_e = sb("tile_e", [1, NT], i32)
        flat = pt.rearrange("p a b c d -> p (a b c d)")
        gu_raw = flat[:, 0:NX * 512]
        wp_raw = flat[:, NX * 512:NX * 512 + WP]
        cmp_ = hid.rearrange("p a n -> p (a n)").rearrange("p (f t e) -> p f t e", f=NE, t=T)
        cmp_n = hid.rearrange("p a n -> p (a n)")[:, 0:NE * 16].rearrange("p (e j) -> p e j", e=NE)
        cmp_t = hid.rearrange("p a n -> p (a n)")[:, 128:128 + NT * NE].rearrange("p (i e) -> p i e", e=NE)
        xn = tile_buf[:, :].rearrange("p (t d) -> p t d", t=T)
        xs_t = tile_buf[:, 0:1024].rearrange("p (a j d) -> p a j d", a=2, j=4)
        sg_t = tile_buf[:, 1024:1536].rearrange("p (a n) -> p a n", a=2)
        h_t = tile_buf[:, 1536:2048].rearrange("p (a n) -> p a n", a=2)
        y_got = gu_l.bitcast(fp32)[:, 512:NX * 512].rearrange("p (s t d) -> p s t d", s=2, t=T)
        spare = cx.rearrange("p a n -> p (a n)")
        yb = spare[:, 0:1024].rearrange("p (a n) -> p a n", a=2)
        rt = spare[:, 1024:1536].rearrange("p (a n) -> p a n", a=4)
        small = spare[:, 1536:1664].rearrange("p (a n) -> p a n", a=8)
        st = spare[:, 1664:1760].rearrange("p (t k) -> p t k", t=T)
        mv = spare[:, 1760:1792].rearrange("p (t k) -> p t k", t=T)
        rbias = spare[:, 1792:1800]
        rot = [(t1[:, :], t2[:, :]), (sg[:, 0, :], sg[:, 1, :])]
        fin = cn.rearrange("p t n -> p (t n)")
        ident, tri = cst[:, 0:128], cst[:, 128:256]
        steps, ramp = cst[:, 256:272], cst[0:1, 272:272 + NT]

        sc = ctx.enter_context(nc.psum_tensor("sc", [128, 4, 512], fp32))
        gu_p = ctx.enter_context(nc.psum_tensor("gu_p", [128, 2, 512], fp32))
        acc = ctx.enter_context(nc.psum_tensor("acc", [128, 512], fp32))
        misc = ctx.enter_context(nc.psum_tensor("misc", [128, 512], fp32))

        def sems(names):
            return [sem(n) for n in names.split()]

        ld_x = [sem(f"ld_x{j}") for j in range(4)]
        ld_gu = [sem(f"ld_gu{j}") for j in range(3)]
        ld_xs = [sem(f"ld_xs{j}") for j in range(2)]
        ld_wp, ld_c, ld_rope, ld_dn, ld_rb = sems("ld_wp ld_c ld_rope ld_dn ld_rb")
        dve_chain, one_ok, zero_ok, xs0 = sems("dve_chain one_ok zero_ok xs0")
        var_ok, sd_ok, xn_ok, xt_ok, xh_ok, xl_ok = sems("var_ok sd_ok xn_ok xt_ok xh_ok xl_ok")
        wph_ok, wpl_ok, guh_ok, gul_ok, kone_ok, vone_ok = sems("wph_ok wpl_ok guh_ok gul_ok kone_ok vone_ok")
        lg_ok, en_ok, mask_ok, cnt_ok, pos_ok, te_ok, sent = sems("lg_ok en_ok mask_ok cnt_ok pos_ok te_ok sent")
        v_ok, vall_ok = sems("v_ok vall_ok")
        proj_ok, rope_ok, qk_ok, vh_ok, vl_ok = sems("proj_ok rope_ok qk_ok vh_ok vl_ok")
        vaug_ok = sem("vaug_ok")
        laid = [sem(f"laid{hb}") for hb in range(4)]
        a_ok, mx_ok, mt_ok, nmh_ok, nml_ok = sems("a_ok mx_ok mt_ok nmh_ok nml_ok")
        mrow = [sem(f"mrow{i}") for i in range(2)]
        b_ok, ex_ok, pv_ok, cx_ok, ct_ok, rc_ok, cn_ok = sems("b_ok ex_ok pv_ok cx_ok ct_ok rc_ok cn_ok")
        cnt2_ok, ch_ok, cl_ok, f_ok, ft_ok, o_ok, st_out = sems("cnt2_ok ch_ok cl_ok f_ok ft_ok o_ok st_out")
        g_ok, u_ok, silu_ok, h_ok, down_ok = sems("g_ok u_ok silu_ok h_ok down_ok")
        kept_ok = sem("kept_ok")
        tx_ok, txh_ok, txl_ok, tg_ok, ts_ok, th_ok = sems("tx_ok txh_ok txl_ok tg_ok ts_ok th_ok")
        tht_ok, tt_ok, tdn_ok, ty_ok = sems("tht_ok tt_ok tdn_ok ty_ok")
        y_st = [sem(f"y_st{j}") for j in range(2)]
        got = [sem(f"got{n}") for n in range(NB)]
        sum_ok = sem("sum_ok")

        x_v = x.rearrange("(t p) d -> p t d", p=128)
        out_v = out.rearrange("(t p) d -> p t d", p=128)
        xs_v = xs.rearrange("(i p) d -> p i d", p=128)
        ys_v = ys.rearrange("(i p) d -> p i d", p=128)

        def tok(n):
            return bass.ds(n * BLK, BLK)

        def after(eng, sem_, count):
            if not isinstance(count, int) or count > 0:
                eng.wait_ge(sem_, count)

        def tiles(n):
            return 4 * BATCHES[n] if isinstance(n, int) else 4 * PER

        def batch0(n):
            return sum(BATCHES[:n]) if isinstance(n, int) else (n - 1) * PER

        def rows_bank(b):
            return gu_p[:, 1, :] if b == 0 else acc[:, :]

        def tile_at(n, step):
            steps_of = LAST_STEPS if late(n) else list(range(tiles(n)))
            return steps_of.index(step) if step in steps_of else -1

        def batch_at(n, step):
            i = tile_at(n, step)
            return i // 4 + 1 if i % 4 == 3 and i + 1 < tiles(n) else 0

        def late(n):
            return isinstance(n, int) and n == NB - 1

        def shared_step(n, u):
            if u == 0:
                return STEPS
            return None if late(n) else STEPS + 2

        def shared_banks(n, u):
            return (acc[:, :], misc[:, :]) if u == 1 and not late(n) else (gu_p[:, 0, :], gu_p[:, 1, :])

        def context_bank(n, hb):
            if late(n):
                return (misc[:, :], gu_p[:, 1, :])[hb % 2]
            return (acc[:, :], misc[:, :])[hb % 2]

        vr_banks = [sc[:, 0, :], sc[:, 1, :], sc[:, 2, :], sc[:, 3, :], gu_p[:, 0, :], gu_p[:, 1, :]]
        vr_tiles = [range(3 * j, min(3 * j + 3, T)) for j in range(6)]

        def vr(j, c0, c1):
            n = len(vr_tiles[j])
            return vr_banks[j][:, 0:n * VR].rearrange("p (t c) -> p t c", c=VR)[:, :, c0:c1]

        def proj_banks(n, w):
            return (acc[:, :], misc[:, :]) if w == 1 and isinstance(n, int) and n == 0 else (gu_p[:, 0, :], gu_p[:, 1, :])

        def stored(eng, it, b):
            eng.wait_ge(y_st[b % 2], (batch0(it) // 2 + b // 2 + 1) * 16 if isinstance(it, int) else (it - 1) * 8 * PER + (b // 2 + 1) * 16)

        block = ctx.enter_context(nc.Block())

        @block.sync
        def _(sp):
            for j in range(4):
                sp.dma_start(xr[:, 4 * j:4 * j + 4, :], x_v[:, 4 * j:4 * j + 4, :]).then_inc(ld_x[j], 16)
                if j == 0:
                    sp.dma_start(cst[:, :], shapes).then_inc(ld_c, 16)
            sp.dma_start(rbias[:, :], r_bias.rearrange("(a e) -> a e", a=1).to_broadcast([128, NE])).then_inc(ld_rb, 16)
            sp.dma_start(rope_t[:, :, :], rope).then_inc(ld_rope, 16)
            sp.wait_ge(ld_x[3], 16)
            for j in range(3):
                cols = slice(1536 * j, 1536 * j + 1536)
                sp.dma_start(gu_raw[:, cols], w_gu[:, cols]).then_inc(ld_gu[j], 16)
            sp.wait_ge(zero_ok, 1)
            sp.dma_start(xs_v, mx[:, :].rearrange("p (a d) -> p a d", a=1).to_broadcast([128, NT, 128])).then_inc(xs0, 16)
            sp.dma_start(dn[:, :], w_dn).then_inc(ld_dn, 16)

            def load_rows(q, b):
                sp.dma_start(xs_t[:, b % 2, :, :], xs_v[:, bass.ds(q * 4, 4), :]).then_inc(ld_xs[b % 2], 16)

            def store_rows(q, b):
                sp.wait_ge(ty_ok, q + 1)
                sp.dma_start(ys_v[:, bass.ds(q * 4, 4), :], yb[:, b % 2, :].rearrange("p (j d) -> p j d", j=4)).then_inc(y_st[b % 2], 16)

            def maxima_rows(it, half):
                sp.wait_ge(nmh_ok, it * 2 + half + 1)
                sp.wait_ge(nml_ok, it * 2 + half + 1)
                for hb in (2 * half, 2 * half + 1):
                    for row, part in ((MAX_HIGH, nmh), (MAX_LOW, nml)):
                        sp.dma_start(qst.bitcast(fp32)[row:row + 97:32, hb, :],
                                     part.bitcast(fp32)[16 * hb:16 * hb + 16, :]).then_inc(mrow[half], 16)

            def lay_out(n, hb):
                part = slice(4 * HD * hb, 4 * HD * hb + 4 * HD)
                for w, (dst, terms) in enumerate(((qst, (vh, vh, vl)), (kst, (vh, vl, vh)))):
                    for j, src in enumerate(terms):
                        sp.dma_start(dst.bitcast(fp32)[j:128:ROW_STEP, hb, :], src.bitcast(fp32)[part, w, :]).then_inc(laid[hb], 16)
                sp.dma_start(qst.bitcast(fp32)[ROW_STEP - 1:128:ROW_STEP, hb, :], nil[:, :]).then_inc(laid[hb], 16)

            def body(it, last):
                n = tiles(it) // 4
                for b in range(2, n):
                    sp.wait_ge(tx_ok, batch0(it) + b - 1)
                    load_rows(batch0(it) + b, b)
                if n > 2:
                    store_rows(batch0(it), 0)
                maxima_rows(it, 0)
                for b in range(1 if n > 2 else 0, n):
                    store_rows(batch0(it) + b, b)
                maxima_rows(it, 1)
                def next_rows():
                    for b in range(2):
                        load_rows(batch0(it + 1) + b, b)

                if not last:
                    if not isinstance(it, int):
                        next_rows()
                    sp.wait_ge(vl_ok, it * 2 + 4)
                    for hb in range(4):
                        sp.wait_ge(b_ok, it * 16 + 4 * hb + 4)
                        lay_out(it + 1, hb)
                        if isinstance(it, int) and hb == 2:
                            sp.wait_ge(sent, 16 * 2 * T)
                            next_rows()

            sp.wait_ge(vl_ok, 2)
            sp.wait_ge(kone_ok, 1)
            for hb in range(4):
                lay_out(0, hb)
            body(0, False)
            with sp.Fori(1, NB - 1) as it:
                body(it, False)
            body(NB - 1, True)
            for n in range(NB):
                sp.wait_ge(sum_ok, n + 1)
                sp.dma_start(out_v[:, n * TB:n * TB + TB, :], xr[:, n * TB:n * TB + TB, :]).then_inc(st_out, 16)
            sp.wait_ge(st_out, 16 * NB)

        @block.gpsimd
        def _(pool):
            def rope_sum(n, w):
                pool.wait_ge(rope_ok, n * 2 + w + 1)
                pool.tensor_tensor(rot[w][0], *rot[w], ALU.add).then_inc(qk_ok, 1)

            def low_part(n, w):
                pool.wait_ge(vh_ok, n * 2 + w + 1)
                pool.tensor_tensor(vl[:, w, :], rot[w][0], vh.bitcast(fp32)[:, w, :], ALU.subtract).then_inc(vl_ok, 1)

            def values(n):
                after(pool, pv_ok, n * 4)
                pool.tensor_copy(v_aug[:, :, :, 0:HD], v_all[:, bass.ds(n * TB, TB), :].rearrange("p t (h d) -> p t h d", d=HD)).then_inc(vaug_ok, 1)

            pool.memset(mx[:, :], 0.0).then_inc(zero_ok, 1)
            pool.memset(one[:, :], 1.0).then_inc(one_ok, 1)
            pool.memset(v_aug[:, :, :, :], 1.0).then_inc(vone_ok, 1)
            pool.memset(nil[:, :], 0.0)
            pool.memset(kst.bitcast(fp32)[:, :, :], 1.0).then_inc(kone_ok, 1)
            pool.wait_ge(wph_ok, 1)
            pool.tensor_tensor(wp_l[:, :], wp_raw, wp_h.bitcast(fp32)[:, :], ALU.subtract).then_inc(wpl_ok, 1)

            def gate_up_low(e):
                pool.wait_ge(guh_ok, e + 1)
                cols = slice(512 * e, 512 * e + 512)
                pool.tensor_tensor(gu_l[:, cols], gu_raw[:, cols], gu_h.bitcast(fp32)[:, cols], ALU.subtract).then_inc(gul_ok, 1)

            gate_up_low(0)
            for w in range(2):
                rope_sum(0, w)
                low_part(0, w)
            for e in range(1, NX):
                gate_up_low(e)
            pool.wait_ge(vone_ok, 1)
            pool.wait_ge(vall_ok, 6)
            values(0)
            pool.wait_ge(xs0, 16)
            pool.wait_ge(pos_ok, 1)
            def send(t):
                for s in range(2):
                    pool.indirect_dma_start(out=xs, out_offset=bass.IndirectOffsetOnAxis(ap=pos[:, s, t:t + 1], axis=0),
                                            in_=xn[:, t, :], in_offset=None).then_inc(sent, 16)

            def body(it, last):
                if not last:
                    rope_sum(it + 1, 0)
                    low_part(it + 1, 0)
                    rope_sum(it + 1, 1)
                    low_part(it + 1, 1)
                    if isinstance(it, int):
                        for t in range(13, T):
                            send(t)
                    values(it + 1)

            for t in range(13):
                send(t)
            body(0, False)
            with pool.Fori(1, NB - 1) as it:
                body(it, False)
            stored(pool, NB - 1, 0)
            stored(pool, NB - 1, 1)
            for t in range(T):
                for s in range(2):
                    pool.indirect_dma_start(out=y_got[:, s, t, :], out_offset=None, in_=ys,
                                            in_offset=bass.IndirectOffsetOnAxis(ap=pos[:, s, t:t + 1], axis=0)).then_inc(got[t // TB], 16)

        @block.scalar
        def _(act):
            act.dma_start(wp_raw, w_proj).then_inc(ld_wp, 16)
            act.wait_ge(ld_wp, 16)
            act.activation(wp_h[:, :], wp_raw, ACT.Copy).then_inc(wph_ok, 1)
            act.wait_ge(var_ok, 1)
            act.activation(sm[:, 1, :], sm[:, 0, :], ACT.Sqrt).then_inc(sd_ok, 1)

            def gate_up_high(e):
                act.wait_ge(ld_gu[e // 3], 16)
                cols = slice(512 * e, 512 * e + 512)
                act.activation(gu_h[:, cols], gu_raw[:, cols], ACT.Copy).then_inc(guh_ok, 1)

            for j in range(4):
                act.wait_ge(xt_ok, j + 1)
                act.activation(xh[:, tok(j)], sc[:, j, :], ACT.Copy).then_inc(xh_ok, 1)
            gate_up_high(0)
            gate_up_high(1)

            def high_part(n, w):
                act.wait_ge(qk_ok, n * 2 + w + 1)
                act.activation(vh[:, w, :], rot[w][0], ACT.Copy).then_inc(vh_ok, 1)

            high_part(0, 0)
            gate_up_high(2)
            gate_up_high(3)
            high_part(0, 1)
            act.wait_ge(lg_ok, 6)
            act.activation(rt[:, 1, :], rt[:, 0, :], ACT.Exp, scale=-1.0).then_inc(en_ok, 1)
            for j in range(6):
                act.activation(v_all[:, 3 * j:3 * j + len(vr_tiles[j]), :], vr(j, 0, 128), ACT.Copy).then_inc(vall_ok, 1)
                if j < 5:
                    gate_up_high(4 + j)
            def tile_high(it, b):
                q = batch0(it) + b
                act.wait_ge(tx_ok, q + 1)
                if b >= 2:
                    act.wait_ge(tg_ok, (q - 1) * 4)
                act.activation(xth[:, b % 2, :], rows_bank(b), ACT.Copy).then_inc(txh_ok, 1)

            def tile_silu(it, s):
                i = batch0(it) * 4 + s
                act.wait_ge(tg_ok, i + 1)
                if s >= 2:
                    act.wait_ge(th_ok, i - 1)
                act.activation(sg_t[:, s % 2, :], gu_p[:, s % 2, 0:256], ACT.Silu).then_inc(ts_ok, 1)

            def tile_hidden_t(it, s):
                i = batch0(it) * 4 + s
                act.wait_ge(tht_ok, i + 1)
                if s >= 2:
                    act.wait_ge(tdn_ok, i - 1)
                act.activation(htb[:, s % 2, :], acc[:, 0:256], ACT.Copy).then_inc(tt_ok, 1)

            def tile_out(it, b):
                q = batch0(it) + b
                act.wait_ge(tdn_ok, q * 4 + 4)
                if b >= 2:
                    stored(act, it, b - 2)
                else:
                    act.wait_ge(ct_ok, it * 4)
                act.activation(yb[:, b % 2, :], misc[:, :], ACT.Copy).then_inc(ty_ok, 1)

            def silu(it, u):
                act.wait_ge(g_ok, it * 2 + u + 1)
                act.wait_ge(vl_ok, it * 2 + 2)
                gate = shared_banks(it, u)[0]
                if u == 1 and late(it):
                    act.wait_ge(kept_ok, 1)
                    gate = sg[:, 1, :]
                act.activation(sg[:, u, :], gate, ACT.Silu).then_inc(silu_ok, 1)

            def negate_high(it, half):
                act.wait_ge(mt_ok, it * 2 + half + 1)
                after(act, mrow[half], it * 64)
                rows = slice(32 * half, 32 * half + 32)
                act.activation(nmh[rows, :], sc[rows, 2, 0:128], ACT.Copy, scale=-1.0).then_inc(nmh_ok, 1)

            def project_out(it):
                act.wait_ge(down_ok, it + 1)
                after(act, ft_ok, it)
                act.activation(fin, acc[:, :], ACT.Copy).then_inc(f_ok, 1)

            def body(it, last):
                n = tiles(it)
                for s in range(STEPS + 2):
                    if batch_at(it, s):
                        tile_high(it, batch_at(it, s))
                    if tile_at(it, s) >= 0:
                        tile_silu(it, tile_at(it, s))
                    if s == 0 and n:
                        project_out(it - 1)
                    if tile_at(it, s - 1) >= 0:
                        tile_hidden_t(it, tile_at(it, s - 1))
                    if tile_at(it, s - 2) % 4 == 3 and tile_at(it, s - 2) > 0:
                        tile_out(it, tile_at(it, s - 2) // 4)
                    if s == 8:
                        negate_high(it, 0)
                    if s == shared_step(it, 0):
                        silu(it, 0)
                    if s == shared_step(it, 1):
                        silu(it, 1)
                negate_high(it, 1)
                if shared_step(it, 1) == STEPS + 2:
                    silu(it, 1)
                if isinstance(it, int) and it == 0:
                    act.wait_ge(gul_ok, NX)
                for p in range(16):
                    hb, g = p // 4, p % 4
                    act.wait_ge(b_ok, it * 16 + p + 1)
                    after(act, pv_ok, it * 4 + max(hb - 1, 0))
                    act.activation(pt[:, hb % 2, g, :, :], sc[:, 2 * (p % 2):2 * (p % 2) + 2, :], ACT.Exp, scale=SCALE).then_inc(ex_ok, 1)
                if last:
                    silu(it, 1)
                else:
                    tile_high(it + 1, 0)
                act.wait_ge(cnt2_ok, it + 1)
                act.activation(ch[:, :], misc[:, :], ACT.Copy).then_inc(ch_ok, 1)
            body(0, False)
            with act.Fori(1, NB - 1) as it:
                body(it, False)
            body(NB - 1, True)
            project_out(NB - 1)

        @block.vector
        def _(dve):
            chain = [0]

            def link(ins):
                chain[0] += 1
                ins.then_inc(dve_chain, 1)
                dve.wait_ge(dve_chain, chain[0])

            for t in range(T):
                dve.wait_ge(ld_x[t // 4], 16)
                last_st = dve.bn_stats(st[:, t, :], xr[:, t, :])
            link(last_st)
            for t in range(T):
                last_mv = dve.bn_aggr(mv[:, t, :], st[:, t, :])
            link(last_mv)
            dve.tensor_scalar(sm[:, 0, :], mv[:, :, 1], EPS, None, ALU.add).then_inc(var_ok, 1)
            dve.wait_ge(sd_ok, 1)
            link(dve.reciprocal(sm[:, 2, :], sm[:, 1, :]))
            link(dve.tensor_tensor(sm[:, 1, :], sm[:, 2, :], sm[:, 2, :], ALU.mult))
            link(dve.tensor_tensor(sm[:, 3, :], sm[:, 1, :], sm[:, 0, :], ALU.mult))
            link(dve.tensor_scalar(sm[:, 1, :], sm[:, 3, :], -0.5, 1.5, ALU.mult, ALU.add))
            link(dve.tensor_tensor(sm[:, 3, :], sm[:, 1, :], sm[:, 2, :], ALU.mult))
            for t in range(T):
                dve.tensor_scalar(xn[:, t, :], xr[:, t, :], mv[:, t, 0:1], sm[:, 3, t:t + 1], ALU.subtract, ALU.mult).then_inc(xn_ok, 1)
            for j in range(4):
                dve.wait_ge(xh_ok, j + 1)
                dve.tensor_tensor(xl[:, tok(j)], sc[:, j, :], xh.bitcast(fp32)[:, tok(j)], ALU.subtract).then_inc(xl_ok, 1)

            def rotate(n, w):
                dve.wait_ge(proj_ok, n * 2 + w + 1)
                if w == 0:
                    after(dve, vl_ok, n * 2)
                elif not (isinstance(n, int) and n == 0):
                    dve.wait_ge(h_ok, n * 2)
                plain, swapped = proj_banks(n, w)
                dve.tensor_tensor(rot[w][0], plain, rope_t[:, 0, :], ALU.mult)
                dve.tensor_tensor(rot[w][1], swapped, rope_t[:, 1, :], ALU.mult).then_inc(rope_ok, 1)

            def high_part(n, w):
                dve.wait_ge(qk_ok, n * 2 + w + 1)
                if not (isinstance(n, int) and n == 0):
                    for hb in range(4):
                        dve.wait_ge(laid[hb], n * LAID)
                dve.tensor_copy(vh[:, w, :], rot[w][0]).then_inc(vh_ok, 1)

            te = lambda a: a.rearrange("p (t e) -> p t e", t=T)
            et = lambda a: a.rearrange("p (e t) -> p e t", e=NE)
            per_t = lambda a: a.rearrange("p e t -> p t e")

            dve.wait_ge(ld_rope, 16)
            rotate(0, 0)
            rotate(0, 1)
            dve.wait_ge(ld_rb, 16)
            for j, tt in enumerate(vr_tiles):
                dve.wait_ge(v_ok, j + 1)
                bias_b = rbias[:, :].rearrange("p (a e) -> p a e", a=1).to_broadcast([128, len(tt), NE])
                dve.tensor_tensor(te(rt[:, 0, :])[:, tt[0]:tt[0] + len(tt), :], vr(j, 128, VR), bias_b, ALU.add).then_inc(lg_ok, 1)
            dve.wait_ge(en_ok, 1)
            link(dve.tensor_scalar(rt[:, 2, :], rt[:, 1, :], 1.0, None, ALU.add))
            link(dve.reciprocal(rt[:, 3, :], rt[:, 2, :]))
            prob = te(rt[:, 3, :])
            for f in range(NE):
                own = prob[:, :, f:f + 1]
                if f > 0:
                    last_c = dve.tensor_tensor(cmp_[:, f, :, 0:f], own.to_broadcast([128, T, f]), prob[:, :, 0:f], ALU.is_gt)
                last_c = dve.tensor_tensor(cmp_[:, f, :, f:NE], own.to_broadcast([128, T, NE - f]), prob[:, :, f:NE], ALU.is_ge)
            link(last_c)
            link(dve.tensor_reduce(te(rt[:, 0, :]), cmp_.rearrange("p f t e -> p t e f"), AX.X, ALU.add))
            dve.tensor_scalar(per_t(et(rt[:, 1, :])), te(rt[:, 0, :]), 2.5, None, ALU.is_lt).then_inc(mask_ok, 1)
            dve.wait_ge(mask_ok, 1)
            link(dve.tensor_tensor(per_t(et(rt[:, 2, :])), per_t(et(rt[:, 1, :])), prob, ALU.mult))
            link(dve.tensor_reduce(small[:, 0, :], per_t(et(rt[:, 2, :])), AX.X, ALU.add))
            link(dve.reciprocal(small[:, 1, :], small[:, 0, :]))
            share = small[:, 1, :].rearrange("p (a t) -> p a t", a=1).to_broadcast([128, NE, T])
            link(dve.tensor_tensor(et(rt[:, 2, :]), et(rt[:, 2, :]), share, ALU.mult))
            dve.wait_ge(cnt_ok, 1)
            counts, upto, place = rt[:, 3, :], rt[:, 0, :], hid.rearrange("p a n -> p (a n)")
            link(dve.tensor_copy(counts, misc[:, 128:256]))
            link(dve.tensor_tensor_scan(upto, one[:, :], counts, 0.0, ALU.mult, ALU.add))
            n_e, nt_e, end_e, base_e = (small[:, 2 + k, 0:NE] for k in range(4))
            link(dve.tensor_reduce(n_e, et(counts), AX.X, ALU.add))
            over = n_e.rearrange("p (e a) -> p e a", a=1).to_broadcast([128, NE, 16])
            limit = steps.rearrange("p (a j) -> p a j", a=1).to_broadcast([128, NE, 16])
            link(dve.tensor_tensor(cmp_n, over, limit, ALU.is_gt))
            link(dve.tensor_reduce(nt_e, cmp_n, AX.X, ALU.add))
            link(dve.tensor_tensor_scan(end_e, one[:, 0:NE], nt_e, 0.0, ALU.mult, ALU.add))
            ends = end_e[0:1].rearrange("p (a e) -> p a e", a=1).to_broadcast([1, NT, NE])
            link(dve.tensor_tensor(cmp_t[0:1], ends, ramp.rearrange("p (i a) -> p i a", a=1).to_broadcast([1, NT, NE]), ALU.is_le))
            link(dve.tensor_reduce(place[0:1, 512:512 + NT], cmp_t[0:1], AX.X, ALU.add))
            dve.tensor_scalar(tile_e[:, :], place[0:1, 512:512 + NT], float(NE - 1), 1.0, ALU.min, ALU.add).then_inc(te_ok, 1)
            link(dve.tensor_tensor(base_e, end_e, nt_e, ALU.subtract))
            link(dve.scalar_tensor_tensor(out=base_e, in0=base_e, scalar=128.0, in1=n_e, op0=ALU.mult, op1=ALU.add))
            link(dve.tensor_tensor(base_e, base_e, et(upto)[:, :, T - 1], ALU.subtract))
            link(dve.tensor_tensor(upto, upto, counts, ALU.subtract))
            link(dve.tensor_tensor(upto, misc[:, 0:128], upto, ALU.add))
            link(dve.tensor_tensor(et(upto), et(upto), base_e.rearrange("p (e a) -> p e a", a=1).to_broadcast([128, NE, T]), ALU.add))
            link(dve.tensor_tensor(upto, upto, rt[:, 1, :], ALU.mult))
            link(dve.tensor_reduce(small[:, 6, :], per_t(et(upto)), AX.X, ALU.max))
            link(dve.tensor_reduce(small[:, 7, :], per_t(et(upto)), AX.X, ALU.add))
            dve.tensor_copy(pos[:, 1, :], small[:, 6, :])
            dve.tensor_tensor(pos[:, 0, :], small[:, 7, :], small[:, 6, :], ALU.subtract).then_inc(pos_ok, 1)

            def token_weights():
                later = small[:, 6, :].rearrange("p (a t) -> p a t", a=1).to_broadcast([128, NE, T])
                for s, op in enumerate((ALU.is_lt, ALU.is_ge)):
                    link(dve.tensor_tensor(et(counts), et(upto), later, op))
                    link(dve.tensor_tensor(counts, counts, rt[:, 2, :], ALU.mult))
                    link(dve.tensor_reduce(w_tok[:, s, :], per_t(et(counts)), AX.X, ALU.add))

            def tile_low(it, b):
                dve.wait_ge(txh_ok, batch0(it) + b + 1)
                dve.tensor_tensor(xtl[:, b % 2, :], rows_bank(b), xth.bitcast(fp32)[:, b % 2, :], ALU.subtract).then_inc(txl_ok, 1)

            def tile_hidden(it, s):
                i = batch0(it) * 4 + s
                dve.wait_ge(ts_ok, i + 1)
                if s >= 2:
                    dve.wait_ge(tht_ok, i - 1)
                dve.tensor_tensor(h_t[:, s % 2, :], gu_p[:, s % 2, 256:512], sg_t[:, s % 2, :], ALU.mult).then_inc(th_ok, 1)

            def hidden(it, u):
                dve.wait_ge(silu_ok, it * 2 + u + 1)
                dve.wait_ge(u_ok, it * 2 + u + 1)
                up = hid[:, 1, :] if u == 1 and late(it) else shared_banks(it, u)[1]
                dve.tensor_tensor(hid[:, u, :], up, sg[:, u, :], ALU.mult).then_inc(h_ok, 1)

            def maxima(it, a):
                dve.wait_ge(a_ok, it * 16 + a + 1)
                dve.tensor_reduce(mx[:, 4 * a:4 * a + 4], sc[:, 2 * (a % 2):2 * (a % 2) + 2, :].rearrange("p b (q k) -> p (b q) k", q=2),
                                  AX.X, ALU.max).then_inc(mx_ok, 1)

            def negate_low(it, half):
                dve.wait_ge(nmh_ok, it * 2 + half + 1)
                rows = slice(32 * half, 32 * half + 32)
                dve.scalar_tensor_tensor(out=nml[rows, :], in0=sc[rows, 2, 0:128], scalar=-1.0, in1=nmh.bitcast(fp32)[rows, :],
                                         op0=ALU.mult, op1=ALU.subtract).then_inc(nml_ok, 1)

            def finish(it):
                dve.wait_ge(ft_ok, it + 1)
                mine = xr[:, bass.ds(it * TB, TB), :]
                dve.tensor_tensor(mine, misc[:, :].rearrange("p (t d) -> p t d", t=TB), mine, ALU.add).then_inc(o_ok, 1)

            def body(it, last):
                n = tiles(it)
                for s in range(16):
                    if batch_at(it, s):
                        tile_low(it, batch_at(it, s))
                    if tile_at(it, s) >= 0:
                        tile_hidden(it, tile_at(it, s))
                    if s == 0:
                        if isinstance(it, int) and it == 0:
                            dve.wait_ge(xs0, 16)
                        after(dve, mt_ok, it * 2)
                    if s == 8:
                        dve.wait_ge(mt_ok, it * 2 + 1)
                    maxima(it, s)
                    if s == 8:
                        negate_low(it, 0)
                    if s == 1 and n:
                        finish(it - 1)
                negate_low(it, 1)
                if isinstance(it, int) and it == 0:
                    token_weights()
                hidden(it, 0)
                if last:
                    dve.wait_ge(u_ok, it * 2 + 2)
                    dve.tensor_copy(sg[:, 1, :], gu_p[:, 0, :])
                    dve.tensor_copy(hid[:, 1, :], gu_p[:, 1, :]).then_inc(kept_ok, 1)
                else:
                    hidden(it, 1)
                    rotate(it + 1, 0)
                    high_part(it + 1, 0)
                    rotate(it + 1, 1)
                    high_part(it + 1, 1)
                if n:
                    stored(dve, it, n // 4 - 2)
                    stored(dve, it, n // 4 - 1)
                for hb in range(4):
                    dve.wait_ge(pv_ok, it * 4 + hb + 1)
                    after(dve, ct_ok, it * 4)
                    dve.tensor_copy(cx[:, hb, :], context_bank(it, hb)).then_inc(cx_ok, 1)
                    if last and hb in (1, 2):
                        combine(hb - 1)
                if last:
                    hidden(it, 1)
                after(dve, ft_ok, it)
                for t in range(TB):
                    dve.wait_ge(ct_ok, it * 4 + t + 1)
                    by_head = sc[:, t, :].rearrange("p (b g c) -> p b g c", g=4, c=32)
                    dve.reciprocal(rc[:, t, :].rearrange("p (b g) -> p b g", g=4), by_head[:, :, :, HD]).then_inc(rc_ok, 1)
                    dve.wait_ge(rc_ok, it * 4 + t + 1)
                    dve.tensor_tensor(cn[:, t, :].rearrange("p (g b d) -> p b g d", g=4, b=4), by_head[:, :, :, 0:HD],
                                      rc[:, t, :].rearrange("p (b g a) -> p b g a", g=4, a=1).to_broadcast([128, 4, 4, HD]),
                                      ALU.mult).then_inc(cn_ok, 1)
                if not last:
                    tile_low(it + 1, 0)
                dve.wait_ge(ch_ok, it + 1)
                dve.tensor_tensor(cl[:, :], misc[:, :], ch.bitcast(fp32)[:, :], ALU.subtract).then_inc(cl_ok, 1)
                if last:
                    combine(NB - 2)

            def combine(n):
                dve.wait_ge(got[n], 16 * 2 * TB)
                dve.wait_ge(o_ok, n + 1)
                for s in range(2):
                    for t in range(n * TB, n * TB + TB):
                        last_s = dve.scalar_tensor_tensor(out=xr[:, t, :], in0=y_got[:, s, t, :], scalar=w_tok[:, s, t:t + 1],
                                                          in1=xr[:, t, :], op0=ALU.mult, op1=ALU.add)
                    if s == 0:
                        link(last_s)
                last_s.then_inc(sum_ok, 1)

            body(0, False)
            with dve.Fori(1, NB - 1) as it:
                body(it, False)
            body(NB - 1, True)
            finish(NB - 1)
            combine(NB - 1)

        @block.tensor
        def _(pe):
            def three(dst, lhs_h, lhs_l, rhs_h, rhs_l, start=True, stop=True):
                pe.matmul(dst, lhs_h, rhs_h, start=start, stop=False)
                pe.matmul(dst, lhs_h, rhs_l, start=False, stop=False)
                return pe.matmul(dst, lhs_l, rhs_h, start=False, stop=stop)

            def wp(c, n=128):
                return wp_h[:, c:c + n], wp_l[:, c:c + n]

            def project(n, w):
                for s, bank in enumerate(proj_banks(n, w)):
                    last = three(bank, *wp((2 * w + s) * 128), xh[:, tok(n)], xl[:, tok(n)])
                last.then_inc(proj_ok, 1)

            pe.wait_ge(ld_c, 16)
            for j in range(4):
                for t in range(4 * j, 4 * j + 4):
                    pe.wait_ge(xn_ok, t + 1)
                    last = pe.transpose(sc[:, j, (t % 4) * 128:(t % 4) * 128 + 128], xn[:, t, :], ident)
                last.then_inc(xt_ok, 1)
            pe.wait_ge(wpl_ok, 1)
            pe.wait_ge(xl_ok, 1)
            project(0, 0)
            project(0, 1)
            for j, tt in enumerate(vr_tiles):
                if j < 4:
                    pe.wait_ge(xl_ok, 4)
                else:
                    pe.wait_ge(rope_ok, 1)
                for k, t in enumerate(tt):
                    cols = slice(128 * t, 128 * t + 128)
                    last = three(vr_banks[j][:, k * VR:k * VR + VR], xh[:, cols], xl[:, cols], *wp(PV, VR))
                last.then_inc(v_ok, 1)
            pe.wait_ge(mask_ok, 1)
            pe.wait_ge(one_ok, 1)
            pe.matmul(misc[:, 0:128], tri, rt[:, 1, :], start=True, stop=True)
            pe.matmul(misc[:, 128:256], one[:, :], rt[:, 1, :], start=True, stop=True).then_inc(cnt_ok, 1)

            def gate_up(it, u):
                gate, up = shared_banks(it, u)
                if u == 0 and tiles(it):
                    pe.wait_ge(th_ok, batch0(it) * 4 + tiles(it))
                elif u == 1 and late(it):
                    pe.wait_ge(h_ok, it * 2 + 1)
                elif u == 1 and tiles(it):
                    pe.wait_ge(tt_ok, batch0(it) * 4 + tiles(it))
                three(gate, gu_h[:, u * 128:u * 128 + 128], gu_l[:, u * 128:u * 128 + 128],
                      xh[:, tok(it)], xl[:, tok(it)]).then_inc(g_ok, 1)
                if u == 1 and not late(it):
                    if tiles(it):
                        pe.wait_ge(ty_ok, batch0(it) + tiles(it) // 4)
                    else:
                        pe.wait_ge(pos_ok, 1)
                o = 256 + u * 128
                three(up, gu_h[:, o:o + 128], gu_l[:, o:o + 128],
                      xh[:, tok(it)], xl[:, tok(it)]).then_inc(u_ok, 1)

            def down(it, u):
                pe.wait_ge(h_ok, it * 2 + u + 1)
                pe.matmul(acc[:, :], dn[:, u * 128:u * 128 + 128], hid[:, u, :], start=(u == 0), stop=False)

            def tile_rows(it, b):
                q = batch0(it) + b
                pe.wait_ge(ld_xs[b % 2], (q // 2 + 1) * 16 if isinstance(it, int) else (it - 1) * 8 * PER + (b // 2 + 1) * 16)
                if b == 0:
                    pe.wait_ge(rope_ok, it * 2 + 2)
                else:
                    pe.wait_ge(tt_ok, batch0(it) * 4 + 4 * b - 2)
                for j in range(4):
                    last = pe.transpose(rows_bank(b)[:, j * 128:j * 128 + 128], xs_t[:, b % 2, j, :], ident)
                last.then_inc(tx_ok, 1)

            def expert(it, s):
                return pe.value_load(tile_e[0:1, bass.ds(batch0(it) * 4 + s, 1)], min_val=1, max_val=NE)

            experts = {}

            def tile_gate_up(it, s):
                i, b, j = batch0(it) * 4 + s, s // 4, s % 4
                if s == 0:
                    experts[0] = expert(it, 0)
                e = experts[s]
                if j == 0:
                    pe.wait_ge(txl_ok, batch0(it) + b + 1)
                if s < 2:
                    pe.wait_ge(txl_ok, batch0(it) + 1)
                else:
                    pe.wait_ge(th_ok, i - 1)
                cols = bass.ds(e * 512, 512)
                three(gu_p[:, s % 2, :], xth[:, b % 2, j * 128:j * 128 + 128], xtl[:, b % 2, j * 128:j * 128 + 128],
                      gu_h[:, cols], gu_l[:, cols]).then_inc(tg_ok, 1)
                if s + 1 < tiles(it):
                    experts[s + 1] = expert(it, s + 1)

            def tile_turn(it, s):
                i = batch0(it) * 4 + s
                pe.wait_ge(th_ok, i + 1)
                if s == 0:
                    pe.wait_ge(f_ok, it)
                elif s % 4 == 2 and s // 4 + 1 < tiles(it) // 4:
                    pe.wait_ge(txl_ok, batch0(it) + (s + 2) // 4 + 1)
                else:
                    pe.wait_ge(tt_ok, i)
                for c in range(2):
                    last = pe.transpose(acc[:, c * 128:c * 128 + 128], h_t[:, s % 2, c * 128:c * 128 + 128], ident)
                last.then_inc(tht_ok, 1)

            def tile_down(it, s):
                i, b, j = batch0(it) * 4 + s, s // 4, s % 4
                e = experts[s]
                pe.wait_ge(tt_ok, i + 1)
                if s == 0:
                    pe.wait_ge(o_ok, it)
                elif j == 0:
                    pe.wait_ge(ty_ok, batch0(it) + b)
                for c in range(2):
                    last = pe.matmul(misc[:, j * 128:j * 128 + 128], htb[:, s % 2, c * 128:c * 128 + 128],
                                     dn[:, bass.ds(e * 256 + c * 128, 128)], start=(c == 0), stop=(c == 1))
                last.then_inc(tdn_ok, 1)

            def scores(it, a):
                g, hb = a % 4, a // 4
                if a % 4 == 0:
                    pe.wait_ge(laid[hb], it * LAID + LAID)
                if a < 2 and isinstance(it, int) and it == 0:
                    pe.wait_ge(vall_ok, 4)
                elif a < 2:
                    pe.wait_ge(cn_ok, it * 4)
                if a == 9:
                    pe.wait_ge(nml_ok, it * 2 + 1)
                if a >= 2:
                    pe.wait_ge(mx_ok, it * 16 + a - 1)
                rows = slice(32 * g, 32 * g + 32)
                for b in range(2):
                    for qt in range(2):
                        q0 = b * SEQ + qt * 128
                        last = pe.matmul(sc[:, 2 * (a % 2) + b, qt * SEQ:qt * SEQ + SEQ], qst[rows, hb, q0:q0 + 128],
                                         kst[rows, hb, b * SEQ:b * SEQ + SEQ], start=True, stop=True)
                last.then_inc(a_ok, 1)

            def scores_t(it, p):
                hb, g = p // 4, p % 4
                if p % 8 == 0:
                    pe.wait_ge(mrow[p // 8], it * 64 + 64)
                if p == 0:
                    pe.wait_ge(mx_ok, it * 16 + 16)
                if p == 1:
                    pe.wait_ge(nml_ok, it * 2 + 2)
                if p >= 2:
                    pe.wait_ge(ex_ok, it * 16 + p - 1)
                rows = slice(32 * g, 32 * g + 32)
                for b in range(2):
                    for kt in range(2):
                        k0 = b * SEQ + kt * 128
                        last = pe.matmul(sc[:, 2 * (p % 2) + b, kt * SEQ:kt * SEQ + SEQ], kst[rows, hb, k0:k0 + 128],
                                         qst[rows, hb, b * SEQ:b * SEQ + SEQ], start=True, stop=True)
                last.then_inc(b_ok, 1)

            def context(it, hb, b, kt):
                bank = context_bank(it, hb)
                if (b, kt) == (0, 0):
                    pe.wait_ge(ex_ok, it * 16 + 4 * hb + 4)
                    context_start(it, hb)
                for g in range(4):
                    last = pe.matmul(bank[32 * g:32 * g + 32, b * SEQ:b * SEQ + SEQ], v_aug[:, 2 * b + kt, 4 * g + hb, :],
                                     pt[:, hb % 2, g, b, kt * SEQ:kt * SEQ + SEQ], start=(kt == 0), stop=(kt == 1))
                if (b, kt) == (1, 1):
                    last.then_inc(pv_ok, 1)

            def context_start(it, hb):
                if hb == 0:
                    pe.wait_ge(vaug_ok, it + 1)
                    if not late(it):
                        pe.wait_ge(silu_ok, it * 2 + 2)
                elif hb == 1 and late(it):
                    pe.wait_ge(kept_ok, 1)
                elif hb == 1:
                    pe.wait_ge(h_ok, it * 2 + 2)
                else:
                    pe.wait_ge(cx_ok, it * 4 + hb - 1)

            def turn_maxima(it, half):
                pe.wait_ge(mx_ok, it * 16 + 8 * half + 8)
                pe.transpose(sc[:, 2, 0:128], mx[:, :], ident).then_inc(mt_ok, 1)

            def project_out(it):
                pe.wait_ge(cl_ok, it + 1)
                three(acc[:, :], *wp(PO), ch[:, :], cl[:, :], start=False).then_inc(down_ok, 1)

            def finish(it):
                pe.wait_ge(f_ok, it + 1)
                for t in range(TB):
                    last = pe.transpose(misc[:, t * 128:t * 128 + 128], fin[:, t * 128:t * 128 + 128], ident)
                last.then_inc(ft_ok, 1)

            def body(it, last_block):
                n = tiles(it)
                for s in range(STEPS + 2):
                    if batch_at(it, s):
                        tile_rows(it, batch_at(it, s))
                    if tile_at(it, s) >= 0:
                        tile_gate_up(it, tile_at(it, s))
                    if s < 16:
                        scores(it, s)
                    if s == 0 and n:
                        project_out(it - 1)
                    if s == 1 and n:
                        finish(it - 1)
                    if s == 8:
                        turn_maxima(it, 0)
                    if batch_at(it, s):
                        tile_down(it, tile_at(it, s - 2))
                    if tile_at(it, s - 1) >= 0:
                        tile_turn(it, tile_at(it, s - 1))
                    if tile_at(it, s - 2) >= 0 and not batch_at(it, s):
                        tile_down(it, tile_at(it, s - 2))
                    if s == shared_step(it, 0) and isinstance(it, int) and it == 0:
                        pe.wait_ge(ld_dn, 16)
                        pe.wait_ge(gul_ok, NX)
                        pe.wait_ge(te_ok, 1)
                        pe.wait_ge(pos_ok, 1)
                    if s == shared_step(it, 0):
                        gate_up(it, 0)
                    if s == shared_step(it, 1):
                        gate_up(it, 1)
                turn_maxima(it, 1)
                if shared_step(it, 1) == STEPS + 2:
                    gate_up(it, 1)
                for p in range(16):
                    scores_t(it, p)
                    if p == 1:
                        if last_block:
                            gate_up(it, 1)
                        else:
                            pe.wait_ge(h_ok, it * 2 + 1)
                            project(it + 1, 0)
                    if p == 3:
                        if last_block:
                            down(it, 0)
                        else:
                            pe.wait_ge(rope_ok, (it + 1) * 2 + 1)
                            project(it + 1, 1)
                    if p >= 4:
                        context(it, p // 4 - 1, p // 2 % 2, p % 2)
                for b in range(2):
                    for kt in range(2):
                        context(it, 3, b, kt)
                if not last_block:
                    pe.wait_ge(cx_ok, it * 4 + 3)
                    down(it, 0)
                    down(it, 1)
                pe.wait_ge(cx_ok, it * 4 + 4)
                for t in range(TB):
                    for hb in range(4):
                        last = pe.transpose(sc[:, t, hb * 128:hb * 128 + 128], cx[:, hb, t * 128:t * 128 + 128], ident)
                    last.then_inc(ct_ok, 1)
                if not last_block:
                    tile_rows(it + 1, 0)
                for t in range(TB):
                    pe.wait_ge(cn_ok, it * 4 + t + 1)
                    last = pe.transpose(misc[:, t * 128:t * 128 + 128], cn[:, t, :], ident)
                last.then_inc(cnt2_ok, 1)
                if last_block:
                    down(it, 1)

            body(0, False)
            with pe.Fori(1, NB - 1) as it:
                body(it, False)
            body(NB - 1, True)
            project_out(NB - 1)
            finish(NB - 1)


def _rope_tables():
    import numpy as np
    hd, seq = 8, 256
    inv = (1.0 / np.float32(10000.0) ** (np.arange(0, hd, 2, dtype=np.float32) / np.float32(hd))).astype(np.float32)
    ang = np.outer(np.arange(seq, dtype=np.float32), inv).astype(np.float32)
    cos, sin = np.cos(ang), np.sin(ang)
    table = np.zeros((128, 2, 512), np.float32)
    for e in range(128):
        i = (e % hd) // 2
        table[e, 0] = np.tile(cos[:, i], 2)
        table[e, 1] = np.tile(sin[:, i], 2) * (1.0 if e % 2 else -1.0)
    return table


def kernel(**inputs):
    import numpy as np
    import concourse.bacc as _bacc
    from concourse import mybir as _mybir
    from concourse.bass_utils import run_bass_kernel_spmd as _run

    g = {k.replace("L0_attn_", "").replace("L0_ffn_", ""): np.asarray(v) for k, v in inputs.items()}
    swap = np.arange(128).reshape(64, 2)[:, ::-1].reshape(-1)
    cols = np.arange(128).reshape(4, 4, 8).transpose(1, 0, 2).reshape(-1)
    w_proj = np.concatenate([g["W_Q"][cols].T, g["W_Q"][swap[cols]].T, g["W_K"][cols].T, g["W_K"][swap[cols]].T, g["W_V"].T,
                             g["router_w"].T, g["W_O"].T], axis=1)
    gate = np.concatenate([g["shared_gate"].T[None], g["gate_w"]], axis=0)
    up = np.concatenate([g["shared_up"].T[None], g["up_w"]], axis=0)
    w_gu = np.concatenate([gate, up], axis=2).transpose(1, 0, 2).reshape(128, -1)
    down = np.concatenate([g["shared_down"].T[None], g["down_w"]], axis=0)
    w_dn = down.reshape(9, 2, 128, 128).transpose(2, 0, 1, 3).reshape(128, -1)
    arrays = {
        "in_x": g["x"].reshape(2048, 128), "in_w_proj": w_proj, "in_w_gu": w_gu, "in_w_dn": w_dn,
        "in_r_bias": g["routing_bias"], "in_rope": _rope_tables(),
        "in_shapes": np.concatenate([np.eye(128), np.triu(np.ones((128, 128)), 1),
                                     np.tile(128.0 * np.arange(16), (128, 1)),
                                     np.tile(np.arange(40.0), (128, 1))], axis=1).astype(np.float32),
    }
    arrays = {n: np.ascontiguousarray(a) for n, a in arrays.items()}
    nc = _bacc.Bacc("TRN2", target_bir_lowering=False, num_devices=1)
    args = [nc.dram_tensor(n, a.shape, _mybir.dt.from_np(a.dtype), kind="ExternalInput").ap() for n, a in arrays.items()]
    out = nc.dram_tensor("out_0", (2048, 128), _mybir.dt.float32, kind="ExternalOutput").ap()
    xs, ys = (nc.dram_tensor(n, (40 * 128, 128), _mybir.dt.float32).ap() for n in ("sorted_rows", "sorted_results"))
    attention_moe_kernel(nc, *args, out, xs, ys)
    r = _run(nc, [arrays], core_ids=[0])
    return r.results[0]["out_0"].reshape(8, 256, 128)
```
